# Optimizing a Trainium2 kernel written in Bass

```python
import numpy as np
import jax
import jax.numpy as jnp

def _softmax(x, axis=-1):
    return jax.nn.softmax(x, axis=axis)

def _gelu(x):
    return jax.nn.gelu(x, approximate=True)

def _silu(x):
    return jax.nn.silu(x)

def _sigmoid(x):
    return jax.nn.sigmoid(x)

def _layernorm(x, axis=-1, eps=1e-05):
    m = jnp.mean(x, axis=axis, keepdims=True)
    v = jnp.var(x, axis=axis, keepdims=True)
    return (x - m) / jnp.sqrt(v + eps)

def _scatter_add(tgt, idx, src, axis=0):
    return tgt.at[idx].add(src)

def _segment_sum(src, seg, n):
    return jax.ops.segment_sum(src, seg, n)
kernel_name = 'mk_conv_seq_d2_conv_nhwc512_r4_1cea1b'

def setup_inputs(seed: int=0):
    np.random.seed(seed)
    _w = jnp.asarray

    def _rec_inputs():
        import jax
        import jax.numpy as jnp
        _gk = jax.random.key(seed)
        x = 7.22e-05 + 1 * jax.random.normal(jax.random.fold_in(_gk, 1), (4, 16, 16, 128), jnp.float32)
        return x
    x = _rec_inputs()

    def _L0_conv_setup():
        import jax, jax.numpy as jnp
        import numpy as np
        B, H, W, C = (4, 16, 16, 128)
        EPS = 0.001
        key = jax.random.key(seed)
        ks = jax.random.split(key, 16)
        c8, c2 = (C // 8, C // 2)
        sc = lambda fan_in: 1.0 / np.sqrt(fan_in)
        inp = {'x': jax.random.normal(ks[0], (B, H, W, C), dtype=jnp.float32), 'wf': jax.random.normal(ks[1], (C, c8), dtype=jnp.float32) * sc(C), 'bf': jnp.zeros((c8,), jnp.float32), 'wg': jax.random.normal(ks[2], (C, c8), dtype=jnp.float32) * sc(C), 'bg': jnp.zeros((c8,), jnp.float32), 'wh': jax.random.normal(ks[3], (C, c2), dtype=jnp.float32) * sc(C), 'bh': jnp.zeros((c2,), jnp.float32), 'wo': jax.random.normal(ks[4], (c2, C), dtype=jnp.float32) * sc(c2), 'bo': jnp.zeros((C,), jnp.float32), 'gamma': jax.random.normal(ks[5], (1,), dtype=jnp.float32) * 0.05, 'wc': jax.random.normal(ks[6], (2 * C, C), dtype=jnp.float32) * sc(2 * C), 'bc': jnp.zeros((C,), jnp.float32), 'bn_scale': jnp.ones((C,), jnp.float32), 'bn_bias': jnp.zeros((C,), jnp.float32), 'bn_mean': jnp.zeros((C,), jnp.float32), 'bn_var': jnp.ones((C,), jnp.float32)}
        return inp
    _L0_conv_all = _L0_conv_setup()
    _L0_conv_in = {k: v for k, v in _L0_conv_all.items() if k in ('wf', 'bf', 'wg', 'bg', 'wh', 'bh', 'wo', 'bo', 'gamma', 'wc', 'bc', 'bn_scale', 'bn_bias', 'bn_mean', 'bn_var')}
    del _L0_conv_all

    def _L1_conv_setup():
        import jax, jax.numpy as jnp
        import numpy as np
        from jax import lax
        N_HEADS = 8
        D_K = 16
        D_V = 16
        TEMP = float(np.sqrt(D_K))

        def avg_pool_3x3_s2_same(x):
            sums = lax.reduce_window(x, 0.0, lax.add, (1, 3, 3, 1), (1, 2, 2, 1), 'SAME')
            ones = jnp.ones(x.shape[:3] + (1,), x.dtype)
            cnt = lax.reduce_window(ones, 0.0, lax.add, (1, 3, 3, 1), (1, 2, 2, 1), 'SAME')
            return sums / cnt

        def conv1x1(x, w, b):
            return jnp.einsum('bhwc,cd->bhwd', x, w) + b
        key = jax.random.key(seed)
        ks = jax.random.split(key, 6)
        C = 128
        s1 = float(np.sqrt(2.0 / (C + D_K)))
        s3 = float(np.sqrt(2.0 / (C + D_V)))
        return {'x': jax.random.normal(ks[0], (4, 16, 16, C), jnp.float32), 'w_q': jax.random.normal(ks[1], (C, N_HEADS * D_K), jnp.float32) * s1, 'b_q': jnp.zeros((N_HEADS * D_K,), jnp.float32), 'w_k': jax.random.normal(ks[2], (C, N_HEADS * D_K), jnp.float32) * s1, 'b_k': jnp.zeros((N_HEADS * D_K,), jnp.float32), 'w_v': jax.random.normal(ks[3], (C, N_HEADS * D_V), jnp.float32) * s3, 'b_v': jnp.zeros((N_HEADS * D_V,), jnp.float32), 'w_o': jax.random.normal(ks[4], (N_HEADS * D_V, C), jnp.float32) * 0.02, 'b_o': jnp.zeros((C,), jnp.float32)}
    _L1_conv_all = _L1_conv_setup()
    _L1_conv_in = {k: v for k, v in _L1_conv_all.items() if k in ('w_q', 'b_q', 'w_k', 'b_k', 'w_v', 'b_v', 'w_o', 'b_o')}
    del _L1_conv_all
    return {'x': x, 'L0_conv_wf': _L0_conv_in['wf'], 'L0_conv_bf': _L0_conv_in['bf'], 'L0_conv_wg': _L0_conv_in['wg'], 'L0_conv_bg': _L0_conv_in['bg'], 'L0_conv_wh': _L0_conv_in['wh'], 'L0_conv_bh': _L0_conv_in['bh'], 'L0_conv_wo': _L0_conv_in['wo'], 'L0_conv_bo': _L0_conv_in['bo'], 'L0_conv_gamma': _L0_conv_in['gamma'], 'L0_conv_wc': _L0_conv_in['wc'], 'L0_conv_bc': _L0_conv_in['bc'], 'L0_conv_bn_scale': _L0_conv_in['bn_scale'], 'L0_conv_bn_bias': _L0_conv_in['bn_bias'], 'L0_conv_bn_mean': _L0_conv_in['bn_mean'], 'L0_conv_bn_var': _L0_conv_in['bn_var'], 'L1_conv_w_q': _L1_conv_in['w_q'], 'L1_conv_b_q': _L1_conv_in['b_q'], 'L1_conv_w_k': _L1_conv_in['w_k'], 'L1_conv_b_k': _L1_conv_in['b_k'], 'L1_conv_w_v': _L1_conv_in['w_v'], 'L1_conv_b_v': _L1_conv_in['b_v'], 'L1_conv_w_o': _L1_conv_in['w_o'], 'L1_conv_b_o': _L1_conv_in['b_o']}

def reference(x, L0_conv_wf, L0_conv_bf, L0_conv_wg, L0_conv_bg, L0_conv_wh, L0_conv_bh, L0_conv_wo, L0_conv_bo, L0_conv_gamma, L0_conv_wc, L0_conv_bc, L0_conv_bn_scale, L0_conv_bn_bias, L0_conv_bn_mean, L0_conv_bn_var, L1_conv_w_q, L1_conv_b_q, L1_conv_w_k, L1_conv_b_k, L1_conv_w_v, L1_conv_b_v, L1_conv_w_o, L1_conv_b_o):
    import jax
    import jax.numpy as jnp

    def _L0_conv_ref(x, wf, bf, wg, bg, wh, bh, wo, bo, gamma, wc, bc, bn_scale, bn_bias, bn_mean, bn_var):
        import jax, jax.numpy as jnp
        import numpy as np
        B, H, W, C = (4, 16, 16, 128)
        EPS = 0.001
        b, h, w, c = x.shape
        n = h * w
        xf = x.reshape(b, n, c)
        f = xf @ wf + bf
        g = xf @ wg + bg
        hv = xf @ wh + bh
        s = jnp.einsum('bnd,bmd->bnm', g, f)
        beta = jax.nn.softmax(s, axis=-1)
        o = jnp.einsum('bnm,bmd->bnd', beta, hv)
        o = o @ wo + bo
        att = gamma * o + xf
        cat = jnp.concatenate([att, xf], axis=-1)
        y = cat @ wc + bc
        y = (y - bn_mean) * (bn_scale / jnp.sqrt(bn_var + EPS)) + bn_bias
        y = jax.nn.relu(y)
        return y.reshape(b, h, w, c)

    def _L1_conv_ref(x, w_q, b_q, w_k, b_k, w_v, b_v, w_o, b_o):
        import jax, jax.numpy as jnp
        import numpy as np
        from jax import lax
        N_HEADS = 8
        D_K = 16
        D_V = 16
        TEMP = float(np.sqrt(D_K))

        def avg_pool_3x3_s2_same(x):
            sums = lax.reduce_window(x, 0.0, lax.add, (1, 3, 3, 1), (1, 2, 2, 1), 'SAME')
            ones = jnp.ones(x.shape[:3] + (1,), x.dtype)
            cnt = lax.reduce_window(ones, 0.0, lax.add, (1, 3, 3, 1), (1, 2, 2, 1), 'SAME')
            return sums / cnt

        def conv1x1(x, w, b):
            return jnp.einsum('bhwc,cd->bhwd', x, w) + b
        BS, H, W, C = x.shape
        residual = x
        qt = conv1x1(x, w_q, b_q).reshape(BS * N_HEADS, H * W, -1)
        xp = avg_pool_3x3_s2_same(x)
        kt = conv1x1(xp, w_k, b_k).reshape(BS * N_HEADS, H * W // 4, -1)
        vt = conv1x1(xp, w_v, b_v).reshape(BS * N_HEADS, H * W // 4, -1)
        attn = jnp.einsum('bnd,bmd->bnm', qt, kt) / TEMP
        attn = jax.nn.softmax(attn, axis=-1)
        out = jnp.einsum('bnm,bmd->bnd', attn, vt)
        out = out.reshape(BS, H, W, -1)
        out = conv1x1(out, w_o, b_o)
        return out + residual

    def _gn(v, G=32, eps=1e-05):
        B_, H_, W_, C_ = v.shape
        g = v.reshape(B_, H_, W_, G, C_ // G)
        m = jnp.mean(g, axis=(1, 2, 4), keepdims=True)
        s = jnp.var(g, axis=(1, 2, 4), keepdims=True)
        return ((g - m) / jnp.sqrt(s + eps)).reshape(v.shape)

    def _ln_c(v, eps=1e-06):
        m = jnp.mean(v, axis=-1, keepdims=True)
        s = jnp.var(v, axis=-1, keepdims=True)
        return (v - m) / jnp.sqrt(s + eps)

    def _ln_t(v, eps=1e-05):
        m = jnp.mean(v, axis=-1, keepdims=True)
        s = jnp.var(v, axis=-1, keepdims=True)
        return (v - m) / jnp.sqrt(s + eps)

    def _to_tokens(v):
        B_, H_, W_, C_ = v.shape
        return v.reshape(B_, H_ * W_, C_)

    def _from_tokens(t, like):
        return t.reshape(like.shape)
    x = _L0_conv_ref(x, L0_conv_wf, L0_conv_bf, L0_conv_wg, L0_conv_bg, L0_conv_wh, L0_conv_bh, L0_conv_wo, L0_conv_bo, L0_conv_gamma, L0_conv_wc, L0_conv_bc, L0_conv_bn_scale, L0_conv_bn_bias, L0_conv_bn_mean, L0_conv_bn_var)
    x = _L1_conv_ref(x, L1_conv_w_q, L1_conv_b_q, L1_conv_w_k, L1_conv_b_k, L1_conv_w_v, L1_conv_b_v, L1_conv_w_o, L1_conv_b_o)
    return x

_drawn_inputs = setup_inputs


def setup_inputs(seed=0):
    import zlib

    import numpy as np

    out = dict(_drawn_inputs(seed))
    spreads = {'L0_conv_bf': (0.0, 2.0),
     'L0_conv_bg': (0.0, 0.8),
     'L0_conv_bh': (0.0, 0.8),
     'L0_conv_bo': (0.0, 2.0),
     'L0_conv_bc': (0.0, 0.1),
     'L0_conv_bn_scale': (1.0, 0.2),
     'L0_conv_bn_bias': (0.0, 0.1),
     'L0_conv_bn_mean': (0.0, 0.1),
     'L0_conv_bn_var': (1.0, 0.2),
     'L1_conv_b_q': (0.0, 0.8),
     'L1_conv_b_k': (0.0, 0.8),
     'L1_conv_b_v': (0.0, 0.8),
     'L1_conv_b_o': (0.0, 0.1)}
    factors = {'L0_conv_wf': 4.202, 'L0_conv_wg': 4.246, 'L0_conv_wh': 4.101, 'L0_conv_wo': 4.215}
    for name, (base, spread) in spreads.items():
        noise = np.random.default_rng([zlib.crc32(name.encode()), seed]).standard_normal(out[name].shape)
        drawn = base * np.exp(spread * noise) if base else spread * noise
        out[name] = jnp.asarray(drawn.astype(out[name].dtype))
    for name, factor in factors.items():
        out[name] = (out[name] * factor).astype(out[name].dtype)
    return out
```

```python
from contextlib import ExitStack

import numpy as np

import concourse.bass as bass
from concourse import mybir

ALU = mybir.AluOpType
ACT = mybir.ActivationFunctionType
F32 = mybir.dt.float32
AX = mybir.AxisListType

P = 128
B, H, W, C = 4, 16, 16, 128
N = H * W
T = N // P
D0 = C // 8
DH = C // 2
HEADS, D = 8, 16
HALF, J = 2, 4
G = C // D
I, E = 4, 2
PIX = N // HEADS
PH, PW = H // 2, W // 2
POOLED = PH * PW
PP = POOLED // HEADS
M = G * PP
Q = 32
VW = D + 1
PITCH = W + 1
EPS = 1e-3
TEMP = float(np.sqrt(D))

EARLY = {"wfg": 48, "bf": 1, "bg": 1, "var": 1}
PREP = {"wo_t": DH, "wc1": C, "wc2": C, "wh_t": C, "gamma": 1, "bc": 1, "bo": 1, "bh": 1, "bn_scale": 1,
        "bn_bias": 1, "bn_mean": 1, "ident": P}
LATE = {"wq": C, "wk": C, "wv": C, "bq": I, "bk": M, "bv": D, "inv_count": POOLED, "keep_e": E, "bo1": 1}


def columns(fields):
    at, out = 0, {}
    for name, width in fields.items():
        out[name] = slice(at, at + width)
        at += width
    return out, at


def build(nc, x_t, early_d, prep_d, late_d, wo1_d, out_t):
    with ExitStack() as ctx:
        def sb(name, *shape):
            return ctx.enter_context(nc.sbuf_tensor(name, [P, *shape], F32))

        def bank(name):
            return ctx.enter_context(nc.psum_tensor(name, [P, 512], F32))

        def sem(name):
            return ctx.enter_context(nc.semaphore(name))

        at_e, n_e = columns(EARLY)
        at_p, n_p = columns(PREP)
        at_l, n_l = columns(LATE)
        early, prep, late = sb("early", n_e), sb("prep", n_p), sb("late", n_l)

        def e_(name, rows=slice(0, P)):
            return early[rows, at_e[name]]

        def p_(name, rows=slice(0, P)):
            return prep[rows, at_p[name]]

        def l_(name, rows=slice(0, P)):
            return late[rows, at_l[name]]

        ident = p_("ident")

        x = sb("x", B, N)
        f = sb("f", B, N)
        g = sb("g", B, N)
        wow = sb("wow", C)
        w3 = sb("w3", C)
        wsum = sb("wsum", C)
        bn = sb("bn", 8)
        val0 = sb("val0", B, T, C)
        nmax0, sum0, rsum0 = sb("nmax0", B, T), sb("sum0", B, T), sb("rsum0", B, T)
        p0 = sb("p0", B, T, N)
        p0n = sb("p0n", B, T, N)
        pt0 = sb("pt0", B, T, N)
        y = sb("y", B, H + 1, PITCH)
        psum_xp = sb("psum_xp", B, POOLED)
        xp = sb("xp", B, POOLED)
        q_heads = sb("q_heads", B, HALF, I, PIX)
        wk_rep = sb("wk_rep", G, P)
        bk_e = sb("bk_e", E, M)
        k_heads = sb("k_heads", B, HALF, E, J, M)
        v_t = sb("v_t", B, HEADS, M)
        v_heads = sb("v_heads", B, HEADS // 2, 2, VW)
        max1 = sb("max1", B, HALF, E * J)
        d1 = sb("d1", B, HALF, E * J, M)
        p1 = sb("p1", B, HALF, E * J * M)
        pt1 = sb("pt1", B, HALF, 4, P)
        rsum1 = sb("rsum1", B, HALF * E * J)
        o_rows = sb("o_rows", B, HALF * E * J, D)
        o_cols = sb("o_cols", B, HALF, I, PIX)
        wo_z = sb("wo_z", I, J, C)
        res = sb("res", B, N)

        bk_fg, bk_s0, bk_pt0, bk_y = bank("bk_fg"), bank("bk_s0"), bank("bk_pt0"), bank("bk_y")
        bk_q, bk_s1a, bk_s1b, bk_k = bank("bk_q"), bank("bk_s1a"), bank("bk_s1b"), bank("bk_k")
        bk_s1 = [bk_s1a, bk_s1b]
        v_ps = bk_q[:, 448:512]
        o_ps = bk_q[:, 0:HALF * E * J * VW]

        x_in = [sem(f"x_in{b}") for b in range(B)]
        early_in, prep_in, late_in, wo1_in = sem("early_in"), sem("prep_in"), sem("late_in"), sem("wo1_in")
        fg_clear, cleared, wsum_made = sem("fg_clear"), sem("cleared"), sem("wsum_made")
        woz_clear, bias_made, wk_made = sem("woz_clear"), sem("bias_made"), sem("wk_made")
        wow_ps, wow_kept, w3_ps, w3_kept, bn_ready = sem("wow_ps"), sem("wow_kept"), sem("w3_ps"), sem("w3_kept"), sem("bn_ready")
        std_ready, dve_step = sem("std_ready"), sem("dve_step")
        fg_ps, f_kept, g_kept, v0_ps, v0_kept = sem("fg_ps"), sem("f_kept"), sem("g_kept"), sem("v0_ps"), sem("v0_kept")
        s0_ps, max0_ready, exp0_done, p0_ready = sem("s0_ps"), sem("max0_ready"), sem("exp0_done"), sem("p0_ready")
        pt0_ps, pt0_kept, y_ps, y_kept = sem("pt0_ps"), sem("pt0_kept"), sem("y_ps"), sem("y_kept")
        pool_sum, pooled, q_ps, q_kept = sem("pool_sum"), sem("pooled"), sem("q_ps"), sem("q_kept")
        k_ps, k_kept, vt_ps, vt_kept, v_done, v_kept = (sem("k_ps"), sem("k_kept"), sem("vt_ps"), sem("vt_kept"),
                                                         sem("v_done"), sem("v_kept"))
        s1_ps, sub1_done, exp1_done, pt1_ps, pt1_kept = (sem("s1_ps"), sem("sub1_done"), sem("exp1_done"),
                                                         sem("pt1_ps"), sem("pt1_kept"))
        o_done, o_kept, ot_ps, ot_kept = sem("o_done"), sem("o_kept"), sem("ot_ps"), sem("ot_kept")
        res_ps, res_kept, stored = sem("res_ps"), sem("res_kept"), sem("stored")

        block = ctx.enter_context(nc.Block())

        @block.sync
        def _(sp):
            sp.dma_start(early[:], early_d).then_inc(early_in, 16)
            sp.dma_start(x[:, 0, :], x_t[:, 0:N]).then_inc(x_in[0], 16)
            sp.dma_start(prep[:], prep_d).then_inc(prep_in, 16)
            for b in range(1, B):
                sp.dma_start(x[:, b, :], x_t[:, b * N:(b + 1) * N]).then_inc(x_in[b], 16)
            sp.dma_start(late[:], late_d).then_inc(late_in, 16)
            sp.wait_ge(woz_clear, 1)
            rows = wo1_d.rearrange("(i e d) c -> e d i c", i=I, e=E)
            for e in range(E):
                for j in range(J):
                    r = (e * J + j) * D
                    sp.dma_start(wo_z[r:r + D, :, j, :], rows[e]).then_inc(wo1_in, 16)
            for b in range(B):
                sp.wait_ge(res_kept, b + 1)
                sp.dma_start(out_t[:, b * N:(b + 1) * N], res[:, b, :]).then_inc(stored, 16)
            sp.wait_ge(stored, 16 * B)

        @block.gpsimd
        def _(pool):
            nc.gpsimd.memset(f[:], 0.0).then_inc(fg_clear, 1)
            nc.gpsimd.memset(g[:], 0.0).then_inc(fg_clear, 1)
            pool.wait_ge(prep_in, 16)
            nc.gpsimd.tensor_tensor(wsum[:], p_("wc1"), p_("wc2"), ALU.add).then_inc(wsum_made, 1)
            nc.gpsimd.memset(y[:], 0.0).then_inc(cleared, 1)
            nc.gpsimd.memset(k_heads[:], 0.0).then_inc(cleared, 1)
            nc.gpsimd.memset(v_heads[:], 0.0).then_inc(cleared, 1)
            nc.gpsimd.memset(wo_z[:], 0.0).then_inc(woz_clear, 1)
            pool.wait_ge(late_in, 16)
            nc.gpsimd.tensor_copy(wk_rep[:].rearrange("c g (r d) -> c g r d", d=D),
                                  l_("wk").rearrange("c (g d) -> c g d", d=D).unsqueeze(2).to_broadcast(
                                      [P, G, P // D, D])).then_inc(wk_made, 1)
            for e in range(E):
                nc.gpsimd.tensor_scalar(bk_e[:, e, :], l_("bk"), l_("keep_e")[:, e:e + 1], None,
                                        ALU.mult).then_inc(bias_made, 1)

        @block.tensor
        def _(pe):
            mm, turn = nc.tensor.matmul, nc.tensor.transpose

            def project_fg(b):
                if b == 0:
                    pe.wait_ge(early_in, 16)
                pe.wait_ge(x_in[b], 16)
                if b >= 1:
                    pe.wait_ge(f_kept, b)
                    pe.wait_ge(g_kept, b)
                mm(bk_fg[0:48, 0:N], e_("wfg"), x[:, b, :], start=True, stop=True).then_inc(fg_ps, 1)

            def weights_1():
                pe.wait_ge(prep_in, 16)
                mm(bk_y[0:DH, 0:C], p_("wo_t"), p_("wc1"), start=True, stop=True).then_inc(wow_ps, 1)

            def weights_2():
                pe.wait_ge(wow_kept, 1)
                mm(bk_y[:, C:2 * C], p_("wh_t", slice(0, DH)), wow[0:DH, :], start=True, stop=True)
                mm(bk_y[:, 2 * C:2 * C + 1], p_("wc1"), p_("bo"), start=True, stop=False)
                mm(bk_y[:, 2 * C:2 * C + 1], wow[0:DH, :], p_("bh", slice(0, DH)), start=False,
                   stop=True).then_inc(w3_ps, 1)

            def values_0(b):
                if b == 0:
                    pe.wait_ge(w3_kept, 1)
                else:
                    pe.wait_ge(pt0_kept, b)
                for t in range(T):
                    last = mm(bk_pt0[:, t * C:(t + 1) * C], x[:, b, t * P:(t + 1) * P], w3[:], start=True, stop=True)
                last.then_inc(v0_ps, 1)

            def scores_0(b):
                if b == 0:
                    pe.wait_ge(fg_clear, 2)
                pe.wait_ge(f_kept, b + 1)
                pe.wait_ge(g_kept, b + 1)
                if b >= 1:
                    pe.wait_ge(exp0_done, T * b)
                for t in range(T):
                    last = mm(bk_s0[:, t * N:(t + 1) * N], g[:, b, t * P:(t + 1) * P], f[:, b, :], start=True, stop=True)
                last.then_inc(s0_ps, 1)

            def turn_0(b, ot_before):
                pe.wait_ge(v0_kept, b + 1)
                if ot_before:
                    pe.wait_ge(ot_kept, ot_before)
                for t in range(T):
                    pe.wait_ge(p0_ready, T * b + t + 1)
                    for m in range(T):
                        last = turn(bk_pt0[:, m * N + t * P:m * N + (t + 1) * P], p0n[:, b, t, m * P:(m + 1) * P], ident)
                last.then_inc(pt0_ps, 1)

            def conv_0(b):
                if b == 0:
                    pe.wait_ge(wsum_made, 1)
                    pe.wait_ge(w3_kept, 2)
                else:
                    pe.wait_ge(vt_kept, b)
                mm(bk_y[:, 0:N], wsum[:], x[:, b, :], start=True, stop=False)
                pe.wait_ge(pt0_kept, b + 1)
                for m in range(T):
                    last = mm(bk_y[:, 0:N], val0[:, b, m, :], pt0[:, b, m, :], start=False, stop=(m == T - 1))
                last.then_inc(y_ps, 1)

            def queries(b):
                if b == 0:
                    pe.wait_ge(late_in, 16)
                else:
                    pe.wait_ge(o_kept, b)
                pe.wait_ge(y_kept, b + 1)
                rows = y[:, b, 0:H, 0:W].rearrange("c (s j r) w -> c s j r w", s=HALF, j=J)
                for i in range(I):
                    for j in range(J):
                        out = bk_q[j * Q:(j + 1) * Q, 0:N].rearrange("c (s i p) -> c s i p", s=HALF, i=I)[:, :, i, :]
                        last = mm(out.rearrange("c s (r w) -> c s r w", r=2), l_("wq")[:, i * Q:(i + 1) * Q],
                                  rows[:, :, j], start=True, stop=True)
                last.then_inc(q_ps, 1)

            def keys(b):
                pe.wait_ge(pooled, b + 1)
                if b == 0:
                    pe.wait_ge(wk_made, 1)
                if b >= 1:
                    pe.wait_ge(res_kept, b)
                out = bk_k[:].rearrange("c (h g p) -> c h g p", h=HEADS, g=G)
                for gk in range(G):
                    last = mm(out[:, :, gk, :], wk_rep[:, gk, :], xp[:, b, :], start=True, stop=True)
                last.then_inc(k_ps, 1)

            def values_1(b):
                pe.wait_ge(pooled, b + 1)
                pe.wait_ge(y_kept, b + 1)
                out = bk_y[0:D, :].rearrange("c (h g p) -> c h g p", h=HEADS, g=G)
                for gv in range(G):
                    last = mm(out[:, :, gv, :], l_("wv")[:, gv * D:(gv + 1) * D], xp[:, b, :], start=True, stop=True)
                last.then_inc(vt_ps, 1)

            def turn_values_1(b):
                pe.wait_ge(vt_kept, b + 1)
                pe.wait_ge(q_kept, b + 1)
                for k in range(HEADS // 2):
                    last = turn(v_ps[:, k * D:(k + 1) * D],
                                v_t[0:D, b, 2 * k:2 * k + 2, :].rearrange("c h m -> c (h m)"), ident[0:D, 0:D])
                last.then_inc(v_done, 1)

            def scores_1(b, s):
                pe.wait_ge(q_kept, b + 1)
                pe.wait_ge(k_kept, b + 1)
                if b >= 1:
                    pe.wait_ge(pt1_kept, HALF * (b - 1) + s + 1)
                mm(bk_s1[s][:, :], q_heads[:, b, s].rearrange("c i p -> c (i p)"),
                   k_heads[:, b, s].rearrange("c e j m -> c (e j m)"), start=True, stop=True).then_inc(s1_ps, 1)

            def turn_1(b, s):
                pe.wait_ge(exp1_done, HALF * b + s + 1)
                for k in range(4):
                    last = turn(bk_s1[s][:, k * P:(k + 1) * P], p1[:, b, s, k * P:(k + 1) * P], ident)
                last.then_inc(pt1_ps, 1)

            def attend_1(b, s):
                pe.wait_ge(v_kept, 2 + 2 * (b + 1))
                pe.wait_ge(pt1_kept, HALF * b + s + 1)
                for k in range(4):
                    at = (s * 4 + k) * 2 * VW
                    last = mm(o_ps[:, at:at + 2 * VW], pt1[:, b, s, k, :],
                              v_heads[:, b, s * 2 + k % 2].rearrange("m h v -> m (h v)"), start=True, stop=True)
                last.then_inc(o_done, 1)

            def turn_output(b, pt0_before):
                pe.wait_ge(o_kept, b + 1)
                pe.wait_ge(pt0_kept, pt0_before)
                for s in range(HALF):
                    last = turn(bk_pt0[:, s * P:(s + 1) * P],
                                o_rows[:, b, s * 8:(s + 1) * 8, :].rearrange("n h v -> n (h v)"), ident)
                last.then_inc(ot_ps, 1)

            def conv_1(b):
                if b == 0:
                    pe.wait_ge(wo1_in, 16 * E * J)
                pe.wait_ge(ot_kept, b + 1)
                pe.wait_ge(k_kept, b + 1)
                out = bk_k[:, 0:N].rearrange("c (s j p) -> c s j p", s=HALF, j=J)
                for j in range(J):
                    for i in range(I):
                        last = mm(out[:, :, j, :], wo_z[:, i, j, :], o_cols[:, b, :, i, :], start=(i == 0),
                                  stop=(i == I - 1))
                last.then_inc(res_ps, 1)

            project_fg(0)
            weights_1()
            scores_0(0)
            weights_2()
            project_fg(1)
            for b in range(B):
                values_0(b)
                turn_0(b, max(b - 1, 0))
                if b + 1 < B:
                    scores_0(b + 1)
                conv_0(b)
                if b + 2 < B:
                    project_fg(b + 2)
                if b >= 1:
                    turn_1(b - 1, 0)
                    turn_1(b - 1, 1)
                    attend_1(b - 1, 0)
                    attend_1(b - 1, 1)
                    turn_output(b - 1, b + 1)
                    conv_1(b - 1)
                queries(b)
                keys(b)
                values_1(b)
                turn_values_1(b)
                scores_1(b, 0)
                scores_1(b, 1)
            turn_1(B - 1, 0)
            turn_1(B - 1, 1)
            attend_1(B - 1, 0)
            attend_1(B - 1, 1)
            turn_output(B - 1, B)
            conv_1(B - 1)

        @block.scalar
        def _(act):
            sc = nc.scalar

            def keep_fg(b):
                act.wait_ge(fg_ps, b + 1)
                if b == 0:
                    act.wait_ge(fg_clear, 2)
                sc.activation(f[0:D0, b, :], bk_fg[0:D0, 0:N], ACT.Identity, bias=e_("bf", slice(0, D0))).then_inc(f_kept, 1)
                sc.activation(g[0:D0, b, :], bk_fg[32:32 + D0, 0:N], ACT.Identity,
                              bias=e_("bg", slice(32, 32 + D0))).then_inc(g_kept, 1)

            def keep_v0(b):
                act.wait_ge(v0_ps, b + 1)
                sc.copy(val0[:, b].rearrange("m t c -> m (t c)"), bk_pt0[:, 0:N]).then_inc(v0_kept, 1)

            def exp_0(b):
                act.wait_ge(max0_ready, b + 1)
                for t in range(T):
                    sc.activation(p0[:, b, t, :], bk_s0[:, t * N:(t + 1) * N], ACT.Exp, bias=nmax0[:, b, t:t + 1],
                                  scale=1.0, accum_out=sum0[:, b, t:t + 1]).then_inc(exp0_done, 1)

            def keep_pt0(b):
                act.wait_ge(pt0_ps, b + 1)
                sc.copy(pt0[:, b].rearrange("m t n -> m (t n)"), bk_pt0[:, :]).then_inc(pt0_kept, 1)

            def norm_relu(b):
                act.wait_ge(y_ps, b + 1)
                if b == 0:
                    act.wait_ge(bn_ready, 2)
                    act.wait_ge(cleared, 1)
                sc.activation(y[:, b, 0:H, 0:W], bk_y[:, 0:N].rearrange("c (h w) -> c h w", h=H), ACT.Relu,
                              bias=bn[:, 7:8], scale=bn[:, 2:3]).then_inc(y_kept, 1)

            def keep_vt(b):
                act.wait_ge(vt_ps, b + 1)
                sc.copy(v_t[0:D, b].rearrange("c h m -> c (h m)"), bk_y[0:D, :]).then_inc(vt_kept, 1)

            def exp_1(b, s):
                act.wait_ge(sub1_done, HALF * b + s + 1)
                sc.activation(p1[:, b, s, :], d1[:, b, s].rearrange("n h m -> n (h m)"), ACT.Exp,
                              scale=1.0 / TEMP).then_inc(exp1_done, 1)

            def keep_pt1(b, s):
                act.wait_ge(pt1_ps, HALF * b + s + 1)
                sc.copy(pt1[:, b, s].rearrange("m k n -> m (k n)"), bk_s1[s][:, :]).then_inc(pt1_kept, 1)

            def keep_ot(b):
                act.wait_ge(ot_ps, b + 1)
                sc.copy(o_cols[:, b].rearrange("c s i p -> c (s i p)"), bk_pt0[:, 0:N]).then_inc(ot_kept, 1)

            act.wait_ge(early_in, 16)
            act.wait_ge(bn_ready, 1)
            sc.activation(bn[:, 1:2], bn[:, 0:1], ACT.Sqrt).then_inc(std_ready, 1)
            keep_fg(0)
            exp_0(0)
            keep_fg(1)
            for b in range(B):
                keep_v0(b)
                keep_pt0(b)
                if b + 1 < B:
                    exp_0(b + 1)
                norm_relu(b)
                if b + 2 < B:
                    keep_fg(b + 2)
                if b >= 1:
                    keep_pt1(b - 1, 0)
                    keep_pt1(b - 1, 1)
                    keep_ot(b - 1)
                keep_vt(b)
                exp_1(b, 0)
                exp_1(b, 1)
            keep_pt1(B - 1, 0)
            keep_pt1(B - 1, 1)
            keep_ot(B - 1)

        @block.vector
        def _(dve):
            v = nc.vector
            steps = [0]

            def step(ins):
                steps[0] += 1
                ins.then_inc(dve_step, 1)
                dve.wait_ge(dve_step, steps[0])

            def max_0(b):
                dve.wait_ge(s0_ps, b + 1)
                v.tensor_reduce(nmax0[:, b, :], bk_s0[:].rearrange("n (t m) -> n t m", t=T), AX.X, ALU.max,
                                negate=True).then_inc(max0_ready, 1)

            def norm_0(b):
                dve.wait_ge(exp0_done, T * (b + 1))
                step(v.reciprocal(rsum0[:, b, :], sum0[:, b, :]))
                for t in range(T):
                    v.tensor_scalar(p0n[:, b, t, :], p0[:, b, t, :], rsum0[:, b, t:t + 1], None,
                                    ALU.mult).then_inc(p0_ready, 1)

            def pool_1(b):
                dve.wait_ge(y_kept, b + 1)
                step(v.tensor_reduce(psum_xp[:, b].rearrange("c (h w) -> c h w", h=PH), windows(y, b), AX.XY, ALU.add))
                v.tensor_tensor(xp[:, b, :], psum_xp[:, b, :], l_("inv_count"), ALU.mult).then_inc(pooled, 1)

            def keep_q(b):
                dve.wait_ge(q_ps, b + 1)
                bias = l_("bq").unsqueeze(1).unsqueeze(3).to_broadcast([P, HALF, I, PIX])
                v.tensor_tensor(q_heads[:, b], bk_q[:, 0:N].rearrange("c (s i p) -> c s i p", s=HALF, i=I), bias,
                                ALU.add).then_inc(q_kept, 1)

            def keep_k(b):
                dve.wait_ge(k_ps, b + 1)
                if b == 0:
                    dve.wait_ge(bias_made, 2)
                    dve.wait_ge(cleared, 2)
                src = bk_k[:].rearrange("c (s j m) -> c s j m", s=HALF, j=J)
                for j in range(J):
                    r = slice(j * Q, (j + 1) * Q)
                    for e in range(E):
                        last = v.scalar_tensor_tensor(
                            out=k_heads[r, b, :, e, j, :], in0=src[r, :, j, :], scalar=l_("keep_e")[r, e:e + 1],
                            in1=bk_e[r, e, :].unsqueeze(1).to_broadcast([Q, HALF, M]), op0=ALU.mult, op1=ALU.add)
                last.then_inc(k_kept, 1)

            def keep_v(b):
                dve.wait_ge(v_done, b + 1)
                if b == 0:
                    dve.wait_ge(cleared, 3)
                    for s in range(2):
                        v.memset(v_heads[64 * s:64 * s + 64, :, :, s, D:VW], 1.0).then_inc(v_kept, 1)
                for s in range(2):
                    r = slice(64 * s, 64 * s + 64)
                    v.tensor_tensor(v_heads[r, b, :, s, 0:D], v_ps[r, :].rearrange("m (k v) -> m k v", v=D),
                                    l_("bv", r).unsqueeze(1).to_broadcast([64, HEADS // 2, D]),
                                    ALU.add).then_inc(v_kept, 1)

            def max_sub_1(b, s):
                dve.wait_ge(s1_ps, HALF * b + s + 1)
                sc1 = bk_s1[s][:].rearrange("n (h m) -> n h m", m=M)
                step(v.tensor_reduce(max1[:, b, s, :], sc1, AX.X, ALU.max))
                v.tensor_tensor(d1[:, b, s], sc1, max1[:, b, s, :].unsqueeze(2).to_broadcast([P, E * J, M]),
                                ALU.subtract).then_inc(sub1_done, 1)

            def norm_1(b):
                dve.wait_ge(o_done, HALF * (b + 1))
                o = o_ps.rearrange("n (h v) -> n h v", v=VW)
                step(v.reciprocal(rsum1[:, b, :], o[:, :, D]))
                v.tensor_tensor(o_rows[:, b], o[:, :, 0:D], rsum1[:, b, :].unsqueeze(2).to_broadcast([P, HALF * E * J, D]),
                                ALU.mult).then_inc(o_kept, 1)

            def result(b):
                dve.wait_ge(res_ps, b + 1)
                v.scalar_tensor_tensor(out=res[:, b, :].rearrange("c (h w) -> c h w", h=H),
                                       in0=bk_k[:, 0:N].rearrange("c (h w) -> c h w", h=H), scalar=l_("bo1"),
                                       in1=y[:, b, 0:H, 0:W], op0=ALU.add, op1=ALU.add).then_inc(res_kept, 1)

            dve.wait_ge(early_in, 16)
            v.tensor_scalar(bn[:, 0:1], e_("var"), EPS, None, ALU.add).then_inc(bn_ready, 1)
            dve.wait_ge(prep_in, 16)
            dve.wait_ge(wow_ps, 1)
            v.tensor_copy(wow[0:DH, :], bk_y[0:DH, 0:C]).then_inc(wow_kept, 1)
            max_0(0)
            dve.wait_ge(w3_ps, 1)
            v.tensor_scalar(w3[:], bk_y[:, C:2 * C], p_("gamma"), None, ALU.mult).then_inc(w3_kept, 1)
            v.tensor_scalar(bn[:, 4:5], bk_y[:, 2 * C:2 * C + 1], p_("gamma"), p_("bc"), ALU.mult,
                            ALU.add).then_inc(w3_kept, 1)
            dve.wait_ge(w3_kept, 2)
            dve.wait_ge(std_ready, 1)
            step(v.reciprocal(bn[:, 3:4], bn[:, 1:2]))
            step(v.tensor_tensor(bn[:, 2:3], bn[:, 3:4], p_("bn_scale"), ALU.mult))
            step(v.tensor_tensor(bn[:, 5:6], bn[:, 4:5], p_("bn_mean"), ALU.subtract))
            v.tensor_scalar(bn[:, 7:8], bn[:, 5:6], bn[:, 2:3], p_("bn_bias"), ALU.mult, ALU.add).then_inc(bn_ready, 1)
            norm_0(0)
            for b in range(B):
                if b + 1 < B:
                    max_0(b + 1)
                    norm_0(b + 1)
                if b >= 1:
                    norm_1(b - 1)
                    result(b - 1)
                if b == 0:
                    dve.wait_ge(late_in, 16)
                pool_1(b)
                keep_q(b)
                keep_k(b)
                keep_v(b)
                max_sub_1(b, 0)
                max_sub_1(b, 1)
            norm_1(B - 1)
            result(B - 1)


def windows(y, b):
    first = y[:, b, 0, 0:1]
    return bass.AP(first.tensor, first.offset,
                   [first.ap[0], (2 * PITCH, PH), (2, PW), (PITCH, 3), (1, 3)])


_IN = ["x_t", "early", "prep", "late", "wo1"]


def packed(fields, given):
    at, n = columns(fields)
    out = np.zeros((P, n), np.float32)
    for name, a in given.items():
        out[:a.shape[0], at[name]] = a
    return out


def kernel(**inputs):
    import concourse.bacc as bacc
    from concourse.bass_utils import run_bass_kernel_spmd

    a = {k: np.asarray(v) for k, v in inputs.items()}
    l0 = {k[8:]: v for k, v in a.items() if k.startswith("L0_conv_")}
    l1 = {k[8:]: v for k, v in a.items() if k.startswith("L1_conv_")}
    zeros = np.zeros((P, 16), np.float32)
    col = lambda v: v.reshape(-1, 1)
    rows, cols = (np.array([3] * (n - 1) + [2]) for n in (PH, PW))
    x_t = np.ascontiguousarray(a["x"].reshape(B * N, C).T)
    given = {
        "early": packed(EARLY, {
            "wfg": np.concatenate([l0["wf"], zeros, l0["wg"]], 1), "bf": col(l0["bf"]),
            "bg": np.concatenate([zeros[:32, :1], col(l0["bg"])]), "var": col(l0["bn_var"])}),
        "prep": packed(PREP, {
            "wo_t": l0["wo"].T, "wc1": l0["wc"][:C], "wc2": l0["wc"][C:], "wh_t": l0["wh"].T,
            "gamma": np.broadcast_to(l0["gamma"].reshape(1, 1), (P, 1)), "bc": col(l0["bc"]), "bo": col(l0["bo"]),
            "bh": col(l0["bh"]), "bn_scale": col(l0["bn_scale"]), "bn_bias": col(l0["bn_bias"]),
            "bn_mean": col(l0["bn_mean"]), "ident": np.eye(P, dtype=np.float32)}),
        "late": packed(LATE, {
            "wq": l1["w_q"], "wk": l1["w_k"], "wv": l1["w_v"],
            "bq": np.tile(l1["b_q"].reshape(I, E * D).T, (J, 1)),
            "bk": np.tile(np.repeat(l1["b_k"].reshape(G, D).T, PP, 1), (J * E, 1)),
            "bv": np.tile(np.repeat(l1["b_v"].reshape(G, D), PP, 0), (2, 1)),
            "inv_count": np.broadcast_to((1.0 / np.outer(rows, cols)).reshape(1, POOLED), (P, POOLED)),
            "keep_e": np.tile(np.repeat(np.eye(E), D, 0), (J, 1)), "bo1": col(l1["b_o"])}),
    }
    arrays = {"x_t": x_t, **given, "wo1": np.ascontiguousarray(l1["w_o"])}
    nc = bacc.Bacc("TRN2", target_bir_lowering=False, num_devices=1)
    args = [nc.dram_tensor(f"in_{k}", arrays[k].shape, F32, kind="ExternalInput").ap() for k in _IN]
    out = nc.dram_tensor("out_t", (C, B * N), F32, kind="ExternalOutput").ap()
    build(nc, *args, out)
    r = run_bass_kernel_spmd(nc, [{f"in_{k}": arrays[k] for k in _IN}], core_ids=[0])
    return np.ascontiguousarray(r.results[0]["out_t"].T).reshape(B, H, W, C)
```

```python
from contextlib import ExitStack

import numpy as np

import concourse.bass as bass
from concourse import mybir

ALU = mybir.AluOpType
ACT = mybir.ActivationFunctionType
F32 = mybir.dt.float32
AX = mybir.AxisListType

P = 128
B, H, W, C = 4, 16, 16, 128
N = H * W
T = N // P
D0 = C // 8
DH = C // 2
HEADS, D = 8, 16
HALF, J = 2, 4
G = C // D
I, E = 4, 2
PIX = N // HEADS
PH, PW = H // 2, W // 2
POOLED = PH * PW
PP = POOLED // HEADS
M = G * PP
Q = 32
VW = D + 1
EPS = 1e-3
WARM = 8
TEMP = float(np.sqrt(D))

FIRST = {"wfg": 48, "bf": 1, "bg": 1, "var": 1, "x0": N}
PREP = {"wo_t": DH, "wc1": C, "wc2": C, "wh_t": C, "gamma": 1, "bc": 1, "bo": 1, "bh": 1, "bn_scale": 1,
        "bn_bias": 1, "bn_mean": 1, "ident": P}
KV = 2 * E * D + D
LATE = {"wkv": G * KV, "wq": C, "wo1": C, "bq": I, "bk": M, "bv": D, "inv_count": POOLED, "bo1": 1}


def columns(fields):
    at, out = 0, {}
    for name, width in fields.items():
        out[name] = slice(at, at + width)
        at += width
    return out, at


def build(nc, first_d, x_d, prep_d, late_d, out_t):
    with ExitStack() as ctx:
        def sb(name, *shape):
            return ctx.enter_context(nc.sbuf_tensor(name, [P, *shape], F32))

        def bank(name):
            return ctx.enter_context(nc.psum_tensor(name, [P, 512], F32))

        def sem(name):
            return ctx.enter_context(nc.semaphore(name))

        at_f, n_f = columns(FIRST)
        at_p, n_p = columns(PREP)
        at_l, n_l = columns(LATE)
        first, prep, late = sb("first", n_f), sb("prep", n_p), sb("late", n_l)

        def f_(name, rows=slice(0, P)):
            return first[rows, at_f[name]]

        def p_(name, rows=slice(0, P)):
            return prep[rows, at_p[name]]

        def l_(name, rows=slice(0, P)):
            return late[rows, at_l[name]]

        ident = p_("ident")

        x_rest = sb("x_rest", B - 1, N)
        f = sb("f", B, N)
        g = sb("g", B, N)
        wow = sb("wow", C)
        w3 = sb("w3", C)
        wsum = sb("wsum", C)
        var_eps, std, rstd, bn_scale, bn_const, bn_mid, bn_bias = (
            sb(n, 1) for n in ("var_eps", "std", "rstd", "bn_scale", "bn_const", "bn_mid", "bn_bias"))
        val0 = sb("val0", B, T, C)
        nmax0, sum0, rsum0 = sb("nmax0", B, T), sb("sum0", B, T), sb("rsum0", B, T)
        p0 = sb("p0", B, T, N)
        p0n = sb("p0n", B, T, N)
        pt0 = sb("pt0", B, T, N)
        y = sb("y", B, H + 1, W)
        xp_sum = sb("xp_sum", B, PH, PW)
        xp = sb("xp", B, POOLED)
        q_raw = sb("q_raw", B, N)
        q_heads = sb("q_heads", B, HALF, I, PIX)
        k_rows = sb("k_rows", B, HALF, J, M)
        k_heads = sb("k_heads", B, HALF, E, J, M)
        v_t = sb("v_t", B, HEADS, M)
        v_heads = sb("v_heads", B, HEADS // 2, 2, VW)
        max1 = sb("max1", B, HALF, E * J)
        d1 = sb("d1", B, HALF, E * J, M)
        p1 = sb("p1", B, HALF, E * J * M)
        pt1 = sb("pt1", B, HALF, 4, P)
        rsum1 = sb("rsum1", B, HALF * E * J)
        o_rows = sb("o_rows", B, HALF, J, E, D)
        o_cols = sb("o_cols", B, N)
        res = sb("res", B, N)
        warm = sb("warm", P)

        bk_fg, bk_s0, bk_pt0, bk_y = bank("bk_fg"), bank("bk_s0"), bank("bk_pt0"), bank("bk_y")
        bk_q, bk_s1a, bk_s1b, bk_k = bank("bk_q"), bank("bk_s1a"), bank("bk_s1b"), bank("bk_k")
        bk_s1 = [bk_s1a, bk_s1b]
        wow_at, w3_at, c_at = slice(0, C), slice(C, 2 * C), slice(2 * C, 2 * C + 1)
        v_ps = bk_y[:, 448:512]
        o_ps = bk_q[:, 0:HALF * E * J * VW]
        V0 = 2 * E * D

        first_in, x_in, prep_in, late_in = sem("first_in"), sem("x_in"), sem("prep_in"), sem("late_in")
        warm_clear, fg_clear, y_clear, k_clear, v_clear, v_ones = (
            sem("warm_clear"), sem("fg_clear"), sem("y_clear"), sem("k_clear"), sem("v_clear"), sem("v_ones"))
        wsum_made, wow_ps, wow_kept, w3_ps, w3_kept, c_kept = (
            sem("wsum_made"), sem("wow_ps"), sem("wow_kept"), sem("w3_ps"), sem("w3_kept"), sem("c_kept"))
        var_ready, std_ready, bn_ready, dve_step = (sem("var_ready"), sem("std_ready"), sem("bn_ready"),
                                                    sem("dve_step"))
        fg_ps, f_kept, g_kept, v0_ps, v0_kept = sem("fg_ps"), sem("f_kept"), sem("g_kept"), sem("v0_ps"), sem("v0_kept")
        s0_ps, max0_ready, exp0_done, p0_ready = sem("s0_ps"), sem("max0_ready"), sem("exp0_done"), sem("p0_ready")
        pt0_ps, pt0_kept, y_ps, y_kept = sem("pt0_ps"), sem("pt0_kept"), sem("y_ps"), sem("y_kept")
        pooled, q_ps, q_turned, q_kept = sem("pooled"), sem("q_ps"), sem("q_turned"), sem("q_kept")
        kv_ps, k_biased, k_dve, k_act, vt_kept, v_ps_done, v_kept = (
            sem("kv_ps"), sem("k_biased"), sem("k_dve"), sem("k_act"), sem("vt_kept"), sem("v_ps_done"),
            sem("v_kept"))
        s1_ps, sub1_done, exp1_done, pt1_ps, pt1_kept, o_ps_done = (
            sem("s1_ps"), sem("sub1_done"), sem("exp1_done"), sem("pt1_ps"), sem("pt1_kept"), sem("o_ps_done"))
        o_kept, o_turned, res_ps, res_kept, stored = (sem("o_kept"), sem("o_turned"), sem("res_ps"),
                                                      sem("res_kept"), sem("stored"))

        def image(b):
            return f_("x0") if b == 0 else x_rest[:, b - 1, :]

        BLOCKS = [(e, j) for e in range(E) for j in range(J)]
        ACT_BLOCKS = 5

        def spread_block(b, e, j):
            return (k_heads[j * Q:(j + 1) * Q, b, :, e, j, :], k_rows[e * Q:(e + 1) * Q, b, :, j, :])

        block = ctx.enter_context(nc.Block())

        @block.sync
        def _(sp):
            sp.dma_start(first[:], first_d).then_inc(first_in, 16)
            sp.dma_start(prep[:], prep_d).then_inc(prep_in, 16)
            sp.dma_start(x_rest[:].rearrange("c b n -> c (b n)"), x_d).then_inc(x_in, 16)
            sp.dma_start(late[:], late_d).then_inc(late_in, 16)
            for b in range(B):
                sp.wait_ge(res_kept, b + 1)
                sp.dma_start(out_t[:, b * N:(b + 1) * N], res[:, b, :]).then_inc(stored, 16)
            sp.wait_ge(stored, 16 * B)

        @block.gpsimd
        def _(pool):
            nc.gpsimd.memset(f[:], 0.0).then_inc(fg_clear, 1)
            nc.gpsimd.memset(g[:], 0.0).then_inc(fg_clear, 1)
            pool.wait_ge(prep_in, 16)
            nc.gpsimd.tensor_tensor(wsum[:], p_("wc1"), p_("wc2"), ALU.add).then_inc(wsum_made, 1)
            nc.gpsimd.memset(y[:, :, H, :], 0.0).then_inc(y_clear, 1)
            nc.gpsimd.memset(v_heads[:], 0.0).then_inc(v_clear, 1)
            nc.gpsimd.memset(k_heads[:], 0.0).then_inc(k_clear, 1)
            pool.wait_ge(late_in, 16)
            bias = l_("bq").unsqueeze(1).unsqueeze(3).to_broadcast([P, HALF, I, PIX])
            for b in range(B):
                pool.wait_ge(q_turned, b + 1)
                nc.gpsimd.tensor_tensor(q_heads[:, b], q_raw[:, b, :].rearrange("c (s i p) -> c s i p", s=HALF, i=I),
                                        bias, ALU.add).then_inc(q_kept, 1)

        @block.tensor
        def _(pe):
            mm, turn = nc.tensor.matmul, nc.tensor.transpose

            def project_fg(b):
                pe.wait_ge(x_in if b else first_in, 16)
                if b >= 1:
                    pe.wait_ge(f_kept, b)
                    pe.wait_ge(g_kept, b)
                mm(bk_fg[0:48, 0:N], f_("wfg"), image(b), start=True, stop=True).then_inc(fg_ps, 1)

            def weights_1():
                pe.wait_ge(prep_in, 16)
                mm(bk_y[0:DH, wow_at], p_("wo_t"), p_("wc1"), start=True, stop=True).then_inc(wow_ps, 1)

            def weights_2():
                pe.wait_ge(wow_kept, 1)
                mm(bk_y[:, w3_at], p_("wh_t", slice(0, DH)), wow[0:DH, :], start=True, stop=True)
                mm(bk_y[:, c_at], p_("wc1"), p_("bo"), start=True, stop=False)
                mm(bk_y[:, c_at], wow[0:DH, :], p_("bh", slice(0, DH)), start=False, stop=True).then_inc(w3_ps, 1)

            def values_0(b):
                if b == 0:
                    pe.wait_ge(w3_kept, 1)
                else:
                    pe.wait_ge(pt0_kept, b)
                for t in range(T):
                    last = mm(bk_pt0[:, t * C:(t + 1) * C], image(b)[:, t * P:(t + 1) * P], w3[:], start=True, stop=True)
                last.then_inc(v0_ps, 1)

            def scores_0(b):
                if b == 0:
                    pe.wait_ge(fg_clear, 2)
                pe.wait_ge(f_kept, b + 1)
                pe.wait_ge(g_kept, b + 1)
                if b >= 1:
                    pe.wait_ge(exp0_done, T * b)
                for t in range(T):
                    last = mm(bk_s0[:, t * N:(t + 1) * N], g[:, b, t * P:(t + 1) * P], f[:, b, :], start=True, stop=True)
                last.then_inc(s0_ps, 1)

            def turn_0(b):
                pe.wait_ge(v0_kept, b + 1)
                for t in range(T):
                    pe.wait_ge(p0_ready, T * b + t + 1)
                    for m in range(T):
                        last = turn(bk_pt0[:, m * N + t * P:m * N + (t + 1) * P], p0n[:, b, t, m * P:(m + 1) * P], ident)
                last.then_inc(pt0_ps, 1)

            def conv_0(b):
                if b == 0:
                    pe.wait_ge(wsum_made, 1)
                    pe.wait_ge(c_kept, 1)
                else:
                    pe.wait_ge(v_kept, 2 * b)
                mm(bk_y[:, 0:N], wsum[:], image(b), start=True, stop=False)
                pe.wait_ge(pt0_kept, b + 1)
                for m in range(T):
                    last = mm(bk_y[:, 0:N], val0[:, b, m, :], pt0[:, b, m, :], start=False, stop=(m == T - 1))
                last.then_inc(y_ps, 1)

            def queries(b):
                if b == 0:
                    pe.wait_ge(late_in, 16)
                if b >= 2:
                    pe.wait_ge(o_kept, b - 1)
                pe.wait_ge(y_kept, b + 1)
                for s in range(HALF):
                    pixels = y[:, b, s * H // 2:(s + 1) * H // 2, :].rearrange("c h w -> c (h w)")
                    last = mm(bk_q[:, s * P:(s + 1) * P], pixels, l_("wq"), start=True, stop=True)
                last.then_inc(q_ps, 1)

            def keys_values(b):
                pe.wait_ge(pooled, b + 1)
                if b >= 2:
                    pe.wait_ge(res_kept, b - 1)
                out = bk_k[0:KV, :].rearrange("c (h g p) -> c h g p", h=HEADS, g=G)
                for gk in range(G):
                    last = mm(out[:, :, gk, :], l_("wkv")[:, gk * KV:(gk + 1) * KV], xp[:, b, :], start=True, stop=True)
                last.then_inc(kv_ps, 1)

            def turn_values(b):
                pe.wait_ge(vt_kept, b + 1)
                pe.wait_ge(y_kept, b + 1)
                for k in range(HEADS // 2):
                    last = turn(v_ps[:, k * D:(k + 1) * D],
                                v_t[V0:V0 + D, b, 2 * k:2 * k + 2, :].rearrange("c h m -> c (h m)"),
                                ident[V0:V0 + D, V0:V0 + D])
                last.then_inc(v_ps_done, 1)

            def scores_1(b, s):
                pe.wait_ge(q_kept, b + 1)
                pe.wait_ge(k_dve, b + 1)
                pe.wait_ge(k_act, b + 1)
                if b >= 1:
                    pe.wait_ge(pt1_kept, HALF * (b - 1) + s + 1)
                mm(bk_s1[s][:, :], q_heads[:, b, s].rearrange("c i p -> c (i p)"),
                   k_heads[:, b, s].rearrange("c e j m -> c (e j m)"), start=True, stop=True).then_inc(s1_ps, 1)

            def turn_1(b, s):
                pe.wait_ge(exp1_done, HALF * b + s + 1)
                for k in range(4):
                    last = turn(bk_s1[s][:, k * P:(k + 1) * P], p1[:, b, s, k * P:(k + 1) * P], ident)
                last.then_inc(pt1_ps, 1)

            def attend_1(b, s):
                pe.wait_ge(v_kept, 2 * (b + 1))
                pe.wait_ge(q_turned, min(b + 2, B))
                pe.wait_ge(pt1_kept, HALF * b + s + 1)
                for k in range(4):
                    at = (s * 4 + k) * 2 * VW
                    last = mm(o_ps[:, at:at + 2 * VW], pt1[:, b, s, k, :],
                              v_heads[:, b, s * 2 + k % 2].rearrange("m h v -> m (h v)"), start=True, stop=True)
                last.then_inc(o_ps_done, 1)

            def conv_1(b):
                pe.wait_ge(o_turned, b + 1)
                pe.wait_ge(k_biased, min(b + 2, B))
                pe.wait_ge(vt_kept, min(b + 2, B))
                mm(bk_k[:, 0:N], l_("wo1"), o_cols[:, b, :], start=True, stop=True).then_inc(res_ps, 1)

            def warm_up():
                pe.wait_ge(warm_clear, 1)
                for _ in range(WARM):
                    mm(bk_k[:, 0:P], warm[:], warm[:], start=True, stop=True)

            warm_up()
            project_fg(0)
            weights_1()
            scores_0(0)
            weights_2()
            project_fg(1)
            values_0(0)
            scores_0(1)
            turn_0(0)
            conv_0(0)
            values_0(1)
            for b in range(B):
                queries(b)
                if b >= 1:
                    turn_1(b - 1, 0)
                    turn_1(b - 1, 1)
                else:
                    project_fg(b + 2)
                if b + 1 < B:
                    turn_0(b + 1)
                keys_values(b)
                if b >= 1:
                    attend_1(b - 1, 0)
                    attend_1(b - 1, 1)
                if b + 2 < B:
                    scores_0(b + 2)
                turn_values(b)
                scores_1(b, 0)
                scores_1(b, 1)
                if b >= 1:
                    conv_1(b - 1)
                if b + 1 < B:
                    conv_0(b + 1)
                if b + 2 < B:
                    values_0(b + 2)
                if b + 3 < B:
                    project_fg(b + 3)
            turn_1(B - 1, 0)
            turn_1(B - 1, 1)
            attend_1(B - 1, 0)
            attend_1(B - 1, 1)
            conv_1(B - 1)

        @block.scalar
        def _(act):
            sc = nc.scalar

            def keep_fg(b):
                act.wait_ge(fg_ps, b + 1)
                if b == 0:
                    act.wait_ge(fg_clear, 2)
                sc.activation(f[0:D0, b, :], bk_fg[0:D0, 0:N], ACT.Identity, bias=f_("bf", slice(0, D0))).then_inc(f_kept, 1)
                sc.activation(g[0:D0, b, :], bk_fg[32:32 + D0, 0:N], ACT.Identity,
                              bias=f_("bg", slice(32, 32 + D0))).then_inc(g_kept, 1)

            def keep_v0(b):
                act.wait_ge(v0_ps, b + 1)
                sc.copy(val0[:, b].rearrange("m t c -> m (t c)"), bk_pt0[:, 0:N]).then_inc(v0_kept, 1)

            def exp_0(b):
                act.wait_ge(max0_ready, b + 1)
                for t in range(T):
                    sc.activation(p0[:, b, t, :], bk_s0[:, t * N:(t + 1) * N], ACT.Exp, bias=nmax0[:, b, t:t + 1],
                                  scale=1.0, accum_out=sum0[:, b, t:t + 1]).then_inc(exp0_done, 1)

            def keep_pt0(b):
                act.wait_ge(pt0_ps, b + 1)
                sc.copy(pt0[:, b].rearrange("m t n -> m (t n)"), bk_pt0[:, :]).then_inc(pt0_kept, 1)

            def norm_relu(b):
                act.wait_ge(y_ps, b + 1)
                if b == 0:
                    act.wait_ge(bn_ready, 1)
                sc.activation(y[:, b, 0:H, :].rearrange("c h w -> c (h w)"), bk_y[:, 0:N], ACT.Relu,
                              bias=bn_bias[:], scale=bn_scale[:]).then_inc(y_kept, 1)

            def keep_vt(b):
                act.wait_ge(kv_ps, b + 1)
                sc.copy(v_t[V0:V0 + D, b].rearrange("c h m -> c (h m)"), bk_k[V0:V0 + D, :]).then_inc(vt_kept, 1)

            def spread_keys(b):
                act.wait_ge(k_biased, b + 1)
                if b == 0:
                    act.wait_ge(k_clear, 1)
                for e, j in BLOCKS[:ACT_BLOCKS]:
                    last = sc.copy(*spread_block(b, e, j))
                last.then_inc(k_act, 1)

            def exp_1(b, s):
                act.wait_ge(sub1_done, HALF * b + s + 1)
                sc.activation(p1[:, b, s, :], d1[:, b, s].rearrange("n h m -> n (h m)"), ACT.Exp,
                              scale=1.0 / TEMP).then_inc(exp1_done, 1)

            def keep_pt1(b, s):
                act.wait_ge(pt1_ps, HALF * b + s + 1)
                sc.copy(pt1[:, b, s].rearrange("m k n -> m (k n)"), bk_s1[s][:, :]).then_inc(pt1_kept, 1)

            act.wait_ge(var_ready, 1)
            sc.activation(std[:], var_eps[:], ACT.Sqrt).then_inc(std_ready, 1)
            keep_fg(0)
            exp_0(0)
            keep_fg(1)
            keep_v0(0)
            exp_0(1)
            keep_pt0(0)
            norm_relu(0)
            keep_v0(1)
            for b in range(B):
                if b >= 1:
                    keep_pt1(b - 1, 0)
                    keep_pt1(b - 1, 1)
                else:
                    keep_fg(b + 2)
                if b + 1 < B:
                    keep_pt0(b + 1)
                keep_vt(b)
                spread_keys(b)
                if b + 2 < B:
                    exp_0(b + 2)
                exp_1(b, 0)
                exp_1(b, 1)
                if b + 1 < B:
                    norm_relu(b + 1)
                if b + 2 < B:
                    keep_v0(b + 2)
                if b + 3 < B:
                    keep_fg(b + 3)
            keep_pt1(B - 1, 0)
            keep_pt1(B - 1, 1)

        @block.vector
        def _(dve):
            v = nc.vector
            steps = [0]

            def step(ins):
                steps[0] += 1
                ins.then_inc(dve_step, 1)
                dve.wait_ge(dve_step, steps[0])

            def max_0(b):
                dve.wait_ge(s0_ps, b + 1)
                v.tensor_reduce(nmax0[:, b, :], bk_s0[:].rearrange("n (t m) -> n t m", t=T), AX.X, ALU.max,
                                negate=True).then_inc(max0_ready, 1)

            def norm_0(b):
                dve.wait_ge(exp0_done, T * (b + 1))
                step(v.reciprocal(rsum0[:, b, :], sum0[:, b, :]))
                for t in range(T):
                    v.tensor_scalar(p0n[:, b, t, :], p0[:, b, t, :], rsum0[:, b, t:t + 1], None,
                                    ALU.mult).then_inc(p0_ready, 1)

            def pool_1(b):
                dve.wait_ge(y_kept, b + 1)
                if b == 0:
                    dve.wait_ge(y_clear, 1)
                v.tensor_reduce(xp_sum[:, b, :, 0:PW - 1], windows(y, b, 0, PW - 1, 3), AX.XY, ALU.add)
                step(v.tensor_reduce(xp_sum[:, b, :, PW - 1:PW], windows(y, b, PW - 1, 1, 2), AX.XY, ALU.add))
                v.tensor_tensor(xp[:, b, :], xp_sum[:, b].rearrange("c h w -> c (h w)"), l_("inv_count"),
                                ALU.mult).then_inc(pooled, 1)

            def turn_q(b):
                dve.wait_ge(q_ps, b + 1)
                v.transpose(q_raw[:, b, :], bk_q[:, 0:N]).then_inc(q_turned, 1)

            def bias_keys(b):
                dve.wait_ge(kv_ps, b + 1)
                step_k = v.tensor_tensor(
                    k_rows[0:V0, b].rearrange("c s j m -> c (s j) m"), bk_k[0:V0, :].rearrange("c (h m) -> c h m", m=M),
                    l_("bk", slice(0, V0)).unsqueeze(1).to_broadcast([V0, HEADS, M]), ALU.add)
                step_k.then_inc(k_biased, 1)

            def spread_keys(b):
                dve.wait_ge(k_biased, b + 1)
                if b == 0:
                    dve.wait_ge(k_clear, 1)
                for e, j in BLOCKS[ACT_BLOCKS:]:
                    last = v.tensor_copy(*spread_block(b, e, j))
                last.then_inc(k_dve, 1)

            def keep_v(b):
                dve.wait_ge(v_ps_done, b + 1)
                if b == 0:
                    dve.wait_ge(v_ones, 2)
                for s in range(2):
                    r = slice(64 * s, 64 * s + 64)
                    v.tensor_tensor(v_heads[r, b, :, s, 0:D], v_ps[r, :].rearrange("m (k v) -> m k v", v=D),
                                    l_("bv", r).unsqueeze(1).to_broadcast([64, HEADS // 2, D]),
                                    ALU.add).then_inc(v_kept, 1)

            def max_sub_1(b, s):
                dve.wait_ge(s1_ps, HALF * b + s + 1)
                sc1 = bk_s1[s][:].rearrange("n (h m) -> n h m", m=M)
                step(v.tensor_reduce(max1[:, b, s, :], sc1, AX.X, ALU.max))
                v.tensor_tensor(d1[:, b, s], sc1, max1[:, b, s, :].unsqueeze(2).to_broadcast([P, E * J, M]),
                                ALU.subtract).then_inc(sub1_done, 1)

            def norm_1(b):
                dve.wait_ge(o_ps_done, HALF * (b + 1))
                o = o_ps.rearrange("n (s e j v) -> n s e j v", s=HALF, e=E, j=J)
                r = rsum1[:, b, :].rearrange("n (s e j) -> n s e j", s=HALF, e=E)
                step(v.reciprocal(rsum1[:, b, :], o_ps.rearrange("n (h v) -> n h v", v=VW)[:, :, D]))
                for s in range(HALF):
                    ins = v.tensor_tensor(o_rows[:, b, s].rearrange("n j e v -> n e j v"), o[:, s, :, :, 0:D],
                                          r[:, s].unsqueeze(3).to_broadcast([P, E, J, D]), ALU.mult)
                ins.then_inc(o_kept, 1)
                dve.wait_ge(o_kept, b + 1)
                v.transpose(o_cols[:, b, :], o_rows[:, b].rearrange("n s j e v -> n (s j e v)")).then_inc(o_turned, 1)

            def result(b):
                dve.wait_ge(res_ps, b + 1)
                v.scalar_tensor_tensor(out=res[:, b, :], in0=bk_k[:, 0:N], scalar=l_("bo1"),
                                       in1=y[:, b, 0:H, :].rearrange("c h w -> c (h w)"), op0=ALU.add,
                                       op1=ALU.add).then_inc(res_kept, 1)

            v.memset(warm[:], 0.0).then_inc(warm_clear, 1)
            dve.wait_ge(first_in, 16)
            v.tensor_scalar(var_eps[:], f_("var"), EPS, None, ALU.add).then_inc(var_ready, 1)
            dve.wait_ge(prep_in, 16)
            dve.wait_ge(wow_ps, 1)
            v.tensor_copy(wow[0:DH, :], bk_y[0:DH, wow_at]).then_inc(wow_kept, 1)
            max_0(0)
            dve.wait_ge(w3_ps, 1)
            v.tensor_scalar(w3[:], bk_y[:, w3_at], p_("gamma"), None, ALU.mult).then_inc(w3_kept, 1)
            norm_0(0)
            v.tensor_scalar(bn_const[:], bk_y[:, c_at], p_("gamma"), p_("bc"), ALU.mult, ALU.add).then_inc(c_kept, 1)
            dve.wait_ge(std_ready, 1)
            step(v.reciprocal(rstd[:], std[:]))
            v.tensor_tensor(bn_scale[:], rstd[:], p_("bn_scale"), ALU.mult)
            dve.wait_ge(c_kept, 1)
            step(v.tensor_tensor(bn_mid[:], bn_const[:], p_("bn_mean"), ALU.subtract))
            v.tensor_scalar(bn_bias[:], bn_mid[:], bn_scale[:], p_("bn_bias"), ALU.mult, ALU.add).then_inc(bn_ready, 1)
            dve.wait_ge(v_clear, 1)
            for s in range(2):
                v.memset(v_heads[64 * s:64 * s + 64, :, :, s, D:VW], 1.0).then_inc(v_ones, 1)
            max_0(1)
            norm_0(1)
            dve.wait_ge(late_in, 16)
            for b in range(B):
                pool_1(b)
                turn_q(b)
                bias_keys(b)
                spread_keys(b)
                if b + 2 < B:
                    max_0(b + 2)
                keep_v(b)
                if b >= 1:
                    norm_1(b - 1)
                max_sub_1(b, 0)
                max_sub_1(b, 1)
                if b >= 1:
                    result(b - 1)
                if b + 2 < B:
                    norm_0(b + 2)
            norm_1(B - 1)
            result(B - 1)


def windows(y, b, at, n, wide):
    start = y[:, b, 0, 2 * at:2 * at + 1]
    return bass.AP(start.tensor, start.offset, [start.ap[0], (2 * W, PH), (2, n), (W, 3), (1, wide)])


_IN = ["first", "x_rest", "prep", "late"]


def packed(fields, given):
    at, n = columns(fields)
    out = np.zeros((P, n), np.float32)
    for name, a in given.items():
        out[:a.shape[0], at[name]] = a
    return out


def kernel(**inputs):
    import concourse.bacc as bacc
    from concourse.bass_utils import run_bass_kernel_spmd

    a = {k: np.asarray(v) for k, v in inputs.items()}
    l0 = {k[8:]: v for k, v in a.items() if k.startswith("L0_conv_")}
    l1 = {k[8:]: v for k, v in a.items() if k.startswith("L1_conv_")}

    def none(*shape):
        return np.zeros(shape, np.float32)

    def col(v):
        return v.reshape(-1, 1)

    sides = [np.array([3] * (n - 1) + [2]) for n in (PH, PW)]
    x_t = a["x"].reshape(B * N, C).T
    wk, wv = (l1[n].reshape(C, G, D) for n in ("w_k", "w_v"))
    bk = np.repeat(l1["b_k"].reshape(G, D).T, PP, 1)
    given = {
        "first": packed(FIRST, {
            "wfg": np.concatenate([l0["wf"], none(C, 32 - D0), l0["wg"]], 1), "bf": col(l0["bf"]),
            "bg": np.concatenate([none(32, 1), col(l0["bg"])]), "var": col(l0["bn_var"]), "x0": x_t[:, :N]}),
        "prep": packed(PREP, {
            "wo_t": l0["wo"].T, "wc1": l0["wc"][:C], "wc2": l0["wc"][C:], "wh_t": l0["wh"].T,
            "gamma": np.broadcast_to(l0["gamma"].reshape(1, 1), (P, 1)), "bc": col(l0["bc"]), "bo": col(l0["bo"]),
            "bh": col(l0["bh"]), "bn_scale": col(l0["bn_scale"]), "bn_bias": col(l0["bn_bias"]),
            "bn_mean": col(l0["bn_mean"]), "ident": np.eye(P, dtype=np.float32)}),
        "late": packed(LATE, {
            "wkv": np.concatenate([wk, none(C, G, D), none(C, G, D), wk, wv], 2).reshape(C, G * KV),
            "wq": l1["w_q"], "wo1": l1["w_o"], "bq": np.tile(l1["b_q"].reshape(I, E * D).T, (J, 1)),
            "bk": np.concatenate([bk, none(D, M), none(D, M), bk]),
            "bv": np.tile(np.repeat(l1["b_v"].reshape(G, D), PP, 0), (2, 1)),
            "inv_count": np.broadcast_to((1.0 / np.outer(*sides)).reshape(1, POOLED), (P, POOLED)),
            "bo1": col(l1["b_o"])}),
    }
    arrays = {**given, "x_rest": np.ascontiguousarray(x_t[:, N:])}
    nc = bacc.Bacc("TRN2", target_bir_lowering=False, num_devices=1)
    args = [nc.dram_tensor(f"in_{k}", arrays[k].shape, F32, kind="ExternalInput").ap() for k in _IN]
    out = nc.dram_tensor("out_t", (C, B * N), F32, kind="ExternalOutput").ap()
    build(nc, *args, out)
    r = run_bass_kernel_spmd(nc, [{f"in_{k}": arrays[k] for k in _IN}], core_ids=[0])
    return np.ascontiguousarray(r.results[0]["out_t"].T).reshape(B, H, W, C)
```

```python
from contextlib import ExitStack

import numpy as np

import concourse.bass as bass
from concourse import mybir

ALU = mybir.AluOpType
ACT = mybir.ActivationFunctionType
F32 = mybir.dt.float32
AX = mybir.AxisListType

P = 128
B, H, W, C = 4, 16, 16, 128
N = H * W
T = N // P
D0 = C // 8
DH = C // 2
HEADS, D = 8, 16
HALF, J = 2, 4
G = C // D
I, E = 4, 2
PIX = N // HEADS
PH, PW = H // 2, W // 2
POOLED = PH * PW
PP = POOLED // HEADS
M = G * PP
Q = 32
VW = D + 1
EPS = 1e-3
WARM = 4
TEMP = float(np.sqrt(D))

FIRST = {"wfg": 48, "bf": 1, "bg": 1, "var": 1, "x0": N}
PREP = {"wo_t": DH, "wc1": C, "wc2": C, "wh_t": C, "gamma": 1, "bc": 1, "bo": 1, "bh": 1, "bn_scale": 1,
        "bn_bias": 1, "bn_mean": 1, "ident": P}
KV = 2 * E * D + D
LATE = {"wkv": G * KV, "wq": C, "wo1": C, "bq": I, "bk": M, "bv": D, "inv_count": POOLED, "bo1": 1}


def columns(fields):
    at, out = 0, {}
    for name, width in fields.items():
        out[name] = slice(at, at + width)
        at += width
    return out, at


def build(nc, first_d, x_d, prep_d, late_d, out_t):
    with ExitStack() as ctx:
        def sb(name, *shape):
            return ctx.enter_context(nc.sbuf_tensor(name, [P, *shape], F32))

        def bank(name):
            return ctx.enter_context(nc.psum_tensor(name, [P, 512], F32))

        def sem(name):
            return ctx.enter_context(nc.semaphore(name))

        at_f, n_f = columns(FIRST)
        at_p, n_p = columns(PREP)
        at_l, n_l = columns(LATE)
        first, prep, late = sb("first", n_f), sb("prep", n_p), sb("late", n_l)

        def f_(name, rows=slice(0, P)):
            return first[rows, at_f[name]]

        def p_(name, rows=slice(0, P)):
            return prep[rows, at_p[name]]

        def l_(name, rows=slice(0, P)):
            return late[rows, at_l[name]]

        ident = p_("ident")

        x_rest = sb("x_rest", B - 1, N)
        f = sb("f", B, N)
        g = sb("g", B, N)
        wow = sb("wow", C)
        w3 = sb("w3", C)
        wsum = sb("wsum", C)
        var_eps, neg_half, rstd, bn_scale, bn_const, bn_mid, bn_bias = (
            sb(n, 1) for n in ("var_eps", "neg_half", "rstd", "bn_scale", "bn_const", "bn_mid", "bn_bias"))
        val0 = sb("val0", B, T, C)
        nmax0, sum0, rsum0 = sb("nmax0", B, T), sb("sum0", B, T), sb("rsum0", B, T)
        p0 = sb("p0", B, T, N)
        p0n = sb("p0n", B, T, N)
        pt0 = sb("pt0", B, T, T, P)
        y = sb("y", B, H + 1, W)
        xp_sum = sb("xp_sum", B, PH, PW)
        xp = sb("xp", B, POOLED)
        q_raw = sb("q_raw", B, N)
        q_heads = sb("q_heads", B, HALF, I, PIX)
        k_rows = sb("k_rows", B, HALF, J, M)
        k_heads = sb("k_heads", B, HALF, E, J, M)
        v_t = sb("v_t", B, HEADS, M)
        v_heads = sb("v_heads", B, HEADS // 2, 2, VW)
        max1 = sb("max1", B, HALF, E * J)
        d1 = sb("d1", B, HALF, E * J, M)
        p1 = sb("p1", B, HALF, E * J * M)
        pt1 = sb("pt1", B, HALF, 4, P)
        rsum1 = sb("rsum1", B, HALF, E * J)
        o_rows = sb("o_rows", B, HALF, J, E, D)
        o_cols = sb("o_cols", B, N)
        res = sb("res", B, N)
        warm, warm_exp = sb("warm", P), sb("warm_exp", 1)

        bk_fg, bk_y, bk_o, bk_k = bank("bk_fg"), bank("bk_y"), bank("bk_o"), bank("bk_k")
        bk_s0 = [bank("bk_s0a"), bank("bk_s0b")]
        bk_s1 = [bank("bk_s1a"), bank("bk_s1b")]
        wow_at, w3_at, c_at = slice(0, C), slice(C, 2 * C), slice(2 * C, 2 * C + 1)
        v0_ps = [bk[:, 0:T * C] for bk in (bk_k, bk_s1[0], bk_s1[0], bk_s1[1])]
        fg_bank = [bk_fg, bk_fg, bk_fg, bk_o]
        v1_ps = bk_y[:, 448:512]

        LAST = B - 1
        o_ps = [[(bk_y if (b, s) == (LAST, 1) else bk_o)[:, s * E * J * VW:(s + 1) * E * J * VW] for s in range(HALF)]
                for b in range(B)]
        res_bank = [bk_s0[0], bk_s0[1], bk_k]
        res_bank_last = [bk_s0[0], bk_fg]
        V0 = 2 * E * D

        first_in, x_in, prep_in, late_in = sem("first_in"), sem("x_in"), sem("prep_in"), sem("late_in")
        warm_clear, fg_clear, y_clear, k_clear, v_clear, v_ones = (
            sem("warm_clear"), sem("fg_clear"), sem("y_clear"), sem("k_clear"), sem("v_clear"), sem("v_ones"))
        wsum_made, wow_ps, wow_kept, w3_ps, w3_kept, c_kept = (
            sem("wsum_made"), sem("wow_ps"), sem("wow_kept"), sem("w3_ps"), sem("w3_kept"), sem("c_kept"))
        rstd_inputs, rstd_ready, bn_ready, dve_step = sem("rstd_inputs"), sem("rstd_ready"), sem("bn_ready"), sem("dve_step")
        fg_ps, f_kept, g_dve, g_act = sem("fg_ps"), sem("f_kept"), sem("g_dve"), sem("g_act")
        v0_done, v0_kept = sem("v0_done"), sem("v0_kept")
        s0_ps, max0_ready, exp0_done = sem("s0_ps"), sem("max0_ready"), sem("exp0_done")
        rsum0_ready, p0_dve, p0_pool = sem("rsum0_ready"), sem("p0_dve"), sem("p0_pool")
        pt0_ps, pt0_kept, y_ps, y_kept = sem("pt0_ps"), sem("pt0_kept"), sem("y_ps"), sem("y_kept")
        pooled, q_ps, q_turned, q_kept = sem("pooled"), sem("q_ps"), sem("q_turned"), sem("q_kept")
        kv_ps, k_biased, k_dve, k_act, vt_kept, v_ps_done, v_kept = (
            sem("kv_ps"), sem("k_biased"), sem("k_dve"), sem("k_act"), sem("vt_kept"), sem("v_ps_done"),
            sem("v_kept"))
        pt1_dve = sem("pt1_dve")
        s1_ps, sub1_done, exp1_done, pt1_ps, pt1_kept, o_ps_done = (
            sem("s1_ps"), sem("sub1_done"), sem("exp1_done"), sem("pt1_ps"), sem("pt1_kept"), sem("o_ps_done"))
        o_kept, o_turned, res_ps, res_kept, stored = (sem("o_kept"), sem("o_turned"), sem("res_ps"),
                                                      sem("res_kept"), sem("stored"))

        assert B == 4 and T == 2

        def image(b):
            return f_("x0") if b == 0 else x_rest[:, b - 1, :]

        BLOCKS = [(e, j) for e in range(E) for j in range(J)]
        ACT_BLOCKS = 4
        DVE_G, DVE_P = 2, 1

        def spread_block(b, e, j):
            return (k_heads[j * Q:(j + 1) * Q, b, :, e, j, :], k_rows[e * Q:(e + 1) * Q, b, :, j, :])

        block = ctx.enter_context(nc.Block())

        @block.sync
        def _(sp):
            sp.dma_start(first[:], first_d).then_inc(first_in, 16)
            sp.dma_start(prep[:], prep_d).then_inc(prep_in, 16)
            sp.dma_start(x_rest[:].rearrange("c b n -> c (b n)"), x_d).then_inc(x_in, 16)
            sp.dma_start(late[:], late_d).then_inc(late_in, 16)
            for b in range(LAST):
                sp.wait_ge(res_kept, b + 1)
                sp.dma_start(out_t[:, b * N:(b + 1) * N], res[:, b, :]).then_inc(stored, 16)
            for s in range(HALF):
                sp.wait_ge(res_kept, LAST + s + 1)
                sp.dma_start(out_t[:, LAST * N + s * P:LAST * N + (s + 1) * P],
                             res[:, LAST, s * P:(s + 1) * P]).then_inc(stored, 16)
            sp.wait_ge(stored, 16 * (LAST + HALF))

        @block.gpsimd
        def _(pool):
            nc.gpsimd.memset(f[:], 0.0).then_inc(fg_clear, 1)
            nc.gpsimd.memset(g[:], 0.0).then_inc(fg_clear, 1)
            nc.gpsimd.memset(neg_half[:], -0.5).then_inc(rstd_inputs, 1)
            pool.wait_ge(first_in, 16)
            nc.gpsimd.tensor_scalar(var_eps[:], f_("var"), EPS, None, ALU.add).then_inc(rstd_inputs, 1)
            pool.wait_ge(rstd_inputs, 2)
            nc.gpsimd.tensor_tensor(rstd[:], var_eps[:], neg_half[:], ALU.pow).then_inc(rstd_ready, 1)
            pool.wait_ge(prep_in, 16)
            nc.gpsimd.tensor_tensor(wsum[:], p_("wc1"), p_("wc2"), ALU.add).then_inc(wsum_made, 1)
            nc.gpsimd.memset(y[:, :, H, :], 0.0).then_inc(y_clear, 1)
            nc.gpsimd.memset(k_heads[:], 0.0).then_inc(k_clear, 1)
            nc.gpsimd.memset(v_heads[:], 0.0).then_inc(v_clear, 1)
            pool.wait_ge(v_clear, 1)
            for s in range(2):
                nc.gpsimd.memset(v_heads[64 * s:64 * s + 64, :, :, s, D:VW], 1.0).then_inc(v_ones, 1)
            pool.wait_ge(v_ones, 2)

            def norm_0(b, t):
                pool.wait_ge(rsum0_ready, T * (b - DVE_P) + t + 1)
                nc.gpsimd.tensor_tensor(p0n[:, b, t, :], p0[:, b, t, :], rsum0[:, b, t:t + 1].to_broadcast([P, N]),
                                        ALU.mult).then_inc(p0_pool, 1)

            def bias_q(b):
                if b == 0:
                    pool.wait_ge(late_in, 16)
                pool.wait_ge(q_turned, b + 1)
                nc.gpsimd.tensor_tensor(q_heads[:, b], q_raw[:, b, :].rearrange("c (s i p) -> c s i p", s=HALF, i=I),
                                        l_("bq").unsqueeze(1).unsqueeze(3).to_broadcast([P, HALF, I, PIX]),
                                        ALU.add).then_inc(q_kept, 1)

            for b in range(B):
                if b + 1 < B:
                    norm_0(b + 1, 0)
                    norm_0(b + 1, 1)
                bias_q(b)

        @block.tensor
        def _(pe):
            mm, turn = nc.tensor.matmul, nc.tensor.transpose

            def project_fg(b):
                pe.wait_ge(x_in if b else first_in, 16)
                if b in (1, 2):
                    pe.wait_ge(f_kept, b)
                    wait_g(b)
                if b == 2:
                    pe.wait_ge(q_turned, 1)
                mm(fg_bank[b][0:48, 0:N], f_("wfg"), image(b), start=True, stop=True).then_inc(fg_ps, 1)

            def wait_g(images):
                pe.wait_ge(g_dve, min(images, DVE_G))
                if images > DVE_G:
                    pe.wait_ge(g_act, images - DVE_G)

            def weights_1():
                pe.wait_ge(prep_in, 16)
                mm(bk_y[0:DH, wow_at], p_("wo_t"), p_("wc1"), start=True, stop=True).then_inc(wow_ps, 1)

            def weights_2():
                pe.wait_ge(wow_kept, 1)
                mm(bk_y[:, w3_at], p_("wh_t", slice(0, DH)), wow[0:DH, :], start=True, stop=True)
                mm(bk_y[:, c_at], p_("wc1"), p_("bo"), start=True, stop=False)
                mm(bk_y[:, c_at], wow[0:DH, :], p_("bh", slice(0, DH)), start=False, stop=True).then_inc(w3_ps, 1)

            def values_0(b):
                if b == 0:
                    pe.wait_ge(w3_kept, 1)
                if b == 2:
                    pe.wait_ge(v0_kept, 2)
                for t in range(T):
                    last = mm(v0_ps[b][:, t * C:(t + 1) * C], image(b)[:, t * P:(t + 1) * P], w3[:], start=True, stop=True)
                last.then_inc(v0_done, 1)

            def scores_0(b, t):
                if t == 0:
                    if b == 0:
                        pe.wait_ge(fg_clear, 2)
                    pe.wait_ge(f_kept, b + 1)
                    wait_g(b + 1)
                if b >= 1:
                    pe.wait_ge(pt0_kept, T * (b - 1) + t + 1)
                mm(bk_s0[t][:, 0:N], g[:, b, t * P:(t + 1) * P], f[:, b, :], start=True, stop=True).then_inc(s0_ps, 1)

            def turn_0(b, t):
                if b == 0:
                    pe.wait_ge(prep_in, 16)
                if b < DVE_P:
                    pe.wait_ge(p0_dve, T * b + t + 1)
                else:
                    pe.wait_ge(p0_pool, T * (b - DVE_P) + t + 1)
                for m in range(T):
                    last = turn(bk_s0[t][:, m * P:(m + 1) * P], p0n[:, b, t, m * P:(m + 1) * P], ident)
                last.then_inc(pt0_ps, 1)

            def conv_0(b):
                if b == 0:
                    pe.wait_ge(wsum_made, 1)
                    pe.wait_ge(c_kept, 1)
                else:
                    pe.wait_ge(v_kept, 2 * b)
                mm(bk_y[:, 0:N], wsum[:], image(b), start=True, stop=False)
                pe.wait_ge(v0_kept, b + 1)
                pe.wait_ge(pt0_kept, T * (b + 1))
                for m in range(T):
                    last = mm(bk_y[:, 0:N].rearrange("c (t n) -> c t n", t=T), val0[:, b, m, :], pt0[:, b, :, m, :],
                              start=False, stop=(m == T - 1))
                last.then_inc(y_ps, 1)

            def queries(b):
                if b == 0:
                    pe.wait_ge(late_in, 16)
                if b <= 1:
                    pe.wait_ge(f_kept, b + 2)
                    wait_g(b + 2)
                else:
                    pe.wait_ge(q_turned, b)
                pe.wait_ge(y_kept, b + 1)
                for s in range(HALF):
                    pixels = y[:, b, s * H // 2:(s + 1) * H // 2, :].rearrange("c h w -> c (h w)")
                    last = mm(bk_fg[:, s * P:(s + 1) * P], pixels, l_("wq"), start=True, stop=True)
                last.then_inc(q_ps, 1)

            def keys_values(b):
                pe.wait_ge(pooled, b + 1)
                if b == 0:
                    pe.wait_ge(v0_kept, 1)
                else:
                    pe.wait_ge(k_biased, b)
                    pe.wait_ge(vt_kept, b)
                out = bk_k[0:KV, :].rearrange("c (h g p) -> c h g p", h=HEADS, g=G)
                for gk in range(G):
                    last = mm(out[:, :, gk, :], l_("wkv")[:, gk * KV:(gk + 1) * KV], xp[:, b, :], start=True, stop=True)
                last.then_inc(kv_ps, 1)

            def turn_values(b):
                pe.wait_ge(vt_kept, b + 1)
                pe.wait_ge(y_kept, b + 1)
                for k in range(HEADS // 2):
                    last = turn(v1_ps[:, k * D:(k + 1) * D],
                                v_t[V0:V0 + D, b, 2 * k:2 * k + 2, :].rearrange("c h m -> c (h m)"),
                                ident[V0:V0 + D, V0:V0 + D])
                last.then_inc(v_ps_done, 1)

            def scores_1(b, s):
                pe.wait_ge(q_kept, b + 1)
                pe.wait_ge(k_dve, b + 1)
                pe.wait_ge(k_act, b + 1)
                if b == 0:
                    pe.wait_ge(v0_kept, (3, 4)[s])
                if b >= 1:
                    pe.wait_ge(pt1_kept, HALF * (b - 1) + s + 1)
                mm(bk_s1[s][:, :], q_heads[:, b, s].rearrange("c i p -> c (i p)"),
                   k_heads[:, b, s].rearrange("c e j m -> c (e j m)"), start=True, stop=True).then_inc(s1_ps, 1)

            def turn_1(b, s):
                pe.wait_ge(exp1_done, HALF * b + s + 1)
                for k in range(4):
                    last = turn(bk_s1[s][:, k * P:(k + 1) * P], p1[:, b, s, k * P:(k + 1) * P], ident)
                last.then_inc(pt1_ps, 1)

            def attend_1(b, s):
                pe.wait_ge(v_kept, 2 * (b + 1))
                if b == 0:
                    pe.wait_ge(f_kept, B)
                    wait_g(B)
                else:
                    pe.wait_ge(o_kept, HALF * b)
                if (b, s) == (LAST, 0):
                    pe.wait_ge(pt1_dve, 1)
                else:
                    pe.wait_ge(pt1_kept, min(HALF * b + s + 1, HALF * B - 1))
                for k in range(4):
                    last = mm(o_ps[b][s][:, k * 2 * VW:(k + 1) * 2 * VW], pt1[:, b, s, k, :],
                              v_heads[:, b, s * 2 + k % 2].rearrange("m h v -> m (h v)"), start=True, stop=True)
                last.then_inc(o_ps_done, 1)

            def conv_1(b):
                pe.wait_ge(o_turned, b + 1)
                if res_bank[b] is bk_k:
                    pe.wait_ge(k_biased, B)
                    pe.wait_ge(vt_kept, B)
                else:
                    pe.wait_ge(pt0_kept, T * B)
                mm(res_bank[b][:, 0:N], l_("wo1"), o_cols[:, b, :], start=True, stop=True).then_inc(res_ps, 1)

            def conv_1_last(s):
                pe.wait_ge(o_turned, LAST + s + 1)
                if s == 0:
                    pe.wait_ge(res_kept, 1)
                else:
                    pe.wait_ge(q_turned, B)
                mm(res_bank_last[s][:, 0:P], l_("wo1"), o_cols[:, LAST, s * P:(s + 1) * P], start=True,
                   stop=True).then_inc(res_ps, 1)

            def warm_up():
                pe.wait_ge(warm_clear, 1)
                for _ in range(WARM):
                    mm(bk_k[:, 0:P], warm[:], warm[:], start=True, stop=True)

            warm_up()
            project_fg(0)
            weights_1()
            scores_0(0, 0)
            scores_0(0, 1)
            weights_2()
            project_fg(1)
            turn_0(0, 0)
            values_0(0)
            turn_0(0, 1)
            values_0(1)
            conv_0(0)
            scores_0(1, 0)
            scores_0(1, 1)
            queries(0)
            values_0(2)
            keys_values(0)
            project_fg(2)
            values_0(3)
            turn_values(0)
            turn_0(1, 0)
            turn_0(1, 1)
            project_fg(3)
            for b in range(B):
                if b >= 1:
                    turn_values(b)
                if 1 <= b < LAST:
                    turn_0(b + 1, 0)
                    turn_0(b + 1, 1)
                scores_1(b, 0)
                scores_1(b, 1)
                if b + 1 < B:
                    conv_0(b + 1)
                if b >= 2:
                    conv_1(b - 2)
                if b + 2 < B:
                    scores_0(b + 2, 0)
                    scores_0(b + 2, 1)
                turn_1(b, 0)
                if b + 1 < B:
                    queries(b + 1)
                if b == LAST:
                    conv_1(LAST - 1)
                turn_1(b, 1)
                if b + 1 < B:
                    keys_values(b + 1)
                attend_1(b, 0)
                attend_1(b, 1)
            conv_1_last(0)
            conv_1_last(1)

        @block.scalar
        def _(act):
            sc = nc.scalar

            def keep_f(b):
                act.wait_ge(fg_ps, b + 1)
                if b == 0:
                    act.wait_ge(fg_clear, 2)
                sc.activation(f[0:D0, b, :], fg_bank[b][0:D0, 0:N], ACT.Identity, bias=f_("bf", slice(0, D0))).then_inc(f_kept, 1)

            def keep_g(b):
                act.wait_ge(fg_ps, b + 1)
                sc.activation(g[0:D0, b, :], fg_bank[b][32:32 + D0, 0:N], ACT.Identity,
                              bias=f_("bg", slice(32, 32 + D0))).then_inc(g_act, 1)

            def keep_v0(b):
                act.wait_ge(v0_done, b + 1)
                sc.copy(val0[:, b].rearrange("m t c -> m (t c)"), v0_ps[b]).then_inc(v0_kept, 1)

            def exp_0(b, t):
                act.wait_ge(max0_ready, T * b + t + 1)
                sc.activation(p0[:, b, t, :], bk_s0[t][:, 0:N], ACT.Exp, bias=nmax0[:, b, t:t + 1],
                              scale=1.0, accum_out=sum0[:, b, t:t + 1]).then_inc(exp0_done, 1)

            def keep_pt0(b, t):
                act.wait_ge(pt0_ps, T * b + t + 1)
                sc.copy(pt0[:, b, t].rearrange("m k n -> m (k n)"), bk_s0[t][:, 0:N]).then_inc(pt0_kept, 1)

            def norm_relu(b):
                act.wait_ge(y_ps, b + 1)
                if b == 0:
                    act.wait_ge(bn_ready, 1)
                sc.activation(y[:, b, 0:H, :].rearrange("c h w -> c (h w)"), bk_y[:, 0:N], ACT.Relu,
                              bias=bn_bias[:], scale=bn_scale[:]).then_inc(y_kept, 1)

            def keep_vt(b):
                act.wait_ge(kv_ps, b + 1)
                sc.copy(v_t[V0:V0 + D, b].rearrange("c h m -> c (h m)"), bk_k[V0:V0 + D, :]).then_inc(vt_kept, 1)

            def spread_keys(b):
                act.wait_ge(k_biased, b + 1)
                if b == 0:
                    act.wait_ge(k_clear, 1)
                for e, j in BLOCKS[:ACT_BLOCKS]:
                    last = sc.copy(*spread_block(b, e, j))
                last.then_inc(k_act, 1)

            def exp_1(b, s):
                act.wait_ge(sub1_done, HALF * b + s + 1)
                sc.activation(p1[:, b, s, :], d1[:, b, s].rearrange("n h m -> n (h m)"), ACT.Exp,
                              scale=1.0 / TEMP).then_inc(exp1_done, 1)

            def keep_pt1(b, s):
                act.wait_ge(pt1_ps, HALF * b + s + 1)
                sc.copy(pt1[:, b, s].rearrange("m k n -> m (k n)"), bk_s1[s][:, :]).then_inc(pt1_kept, 1)

            act.wait_ge(warm_clear, 1)
            sc.activation(warm_exp[:], warm[:, 0:1], ACT.Exp)
            keep_f(0)
            exp_0(0, 0)
            exp_0(0, 1)
            keep_f(1)
            keep_pt0(0, 0)
            keep_v0(0)
            keep_pt0(0, 1)
            keep_v0(1)
            norm_relu(0)
            exp_0(1, 0)
            keep_v0(2)
            exp_0(1, 1)
            keep_vt(0)
            spread_keys(0)
            keep_pt0(1, 0)
            keep_pt0(1, 1)
            keep_v0(3)
            for b in (2, 3):
                keep_g(b)
                keep_f(b)
            for b in range(B):
                if 1 <= b < LAST:
                    keep_pt0(b + 1, 0)
                    keep_pt0(b + 1, 1)
                exp_1(b, 0)
                if b + 1 < B:
                    norm_relu(b + 1)
                exp_1(b, 1)
                if b < LAST:
                    keep_pt1(b, 0)
                if b + 2 < B:
                    exp_0(b + 2, 0)
                    exp_0(b + 2, 1)
                keep_pt1(b, 1)
                if b + 1 < B:
                    keep_vt(b + 1)
                    spread_keys(b + 1)

        @block.vector
        def _(dve):
            v = nc.vector
            steps = [0]

            def step(ins):
                steps[0] += 1
                ins.then_inc(dve_step, 1)
                dve.wait_ge(dve_step, steps[0])

            def keep_g(b):
                dve.wait_ge(fg_ps, b + 1)
                if b == 0:
                    dve.wait_ge(fg_clear, 2)
                v.tensor_scalar(g[0:D0, b, :], bk_fg[32:32 + D0, 0:N], f_("bg", slice(32, 32 + D0)), None,
                                ALU.add).then_inc(g_dve, 1)

            def max_0(b, t):
                dve.wait_ge(s0_ps, T * b + t + 1)
                v.tensor_reduce(nmax0[:, b, t:t + 1], bk_s0[t][:, 0:N], AX.X, ALU.max, negate=True).then_inc(max0_ready, 1)

            def norm_0(b, t):
                dve.wait_ge(exp0_done, T * b + t + 1)
                step(v.reciprocal(rsum0[:, b, t:t + 1], sum0[:, b, t:t + 1]))
                v.tensor_scalar(p0n[:, b, t, :], p0[:, b, t, :], rsum0[:, b, t:t + 1], None,
                                ALU.mult).then_inc(p0_dve, 1)

            def rsum_0(b, t):
                dve.wait_ge(exp0_done, T * b + t + 1)
                v.reciprocal(rsum0[:, b, t:t + 1], sum0[:, b, t:t + 1]).then_inc(rsum0_ready, 1)

            def pool_1(b):
                dve.wait_ge(y_kept, b + 1)
                if b == 0:
                    dve.wait_ge(y_clear, 1)
                v.tensor_reduce(xp_sum[:, b, :, 0:PW - 1], windows(y, b, 0, PW - 1, 3), AX.XY, ALU.add)
                step(v.tensor_reduce(xp_sum[:, b, :, PW - 1:PW], windows(y, b, PW - 1, 1, 2), AX.XY, ALU.add))
                v.tensor_tensor(xp[:, b, :], xp_sum[:, b].rearrange("c h w -> c (h w)"), l_("inv_count"),
                                ALU.mult).then_inc(pooled, 1)

            def turn_q(b):
                dve.wait_ge(q_ps, b + 1)
                v.transpose(q_raw[:, b, :], bk_fg[:, 0:N]).then_inc(q_turned, 1)

            def bias_keys(b):
                dve.wait_ge(kv_ps, b + 1)
                v.tensor_tensor(
                    k_rows[0:V0, b].rearrange("c s j m -> c (s j) m"), bk_k[0:V0, :].rearrange("c (h m) -> c h m", m=M),
                    l_("bk", slice(0, V0)).unsqueeze(1).to_broadcast([V0, HEADS, M]), ALU.add).then_inc(k_biased, 1)

            def spread_keys(b):
                dve.wait_ge(k_biased, b + 1)
                if b == 0:
                    dve.wait_ge(k_clear, 1)
                for e, j in BLOCKS[ACT_BLOCKS:]:
                    last = v.tensor_copy(*spread_block(b, e, j))
                last.then_inc(k_dve, 1)

            def keep_v(b):
                dve.wait_ge(v_ps_done, b + 1)
                if b == 0:
                    dve.wait_ge(v_ones, 2)
                for s in range(2):
                    r = slice(64 * s, 64 * s + 64)
                    v.tensor_tensor(v_heads[r, b, :, s, 0:D], v1_ps[r, :].rearrange("m (k v) -> m k v", v=D),
                                    l_("bv", r).unsqueeze(1).to_broadcast([64, HEADS // 2, D]),
                                    ALU.add).then_inc(v_kept, 1)

            def max_sub_1(b, s):
                dve.wait_ge(s1_ps, HALF * b + s + 1)
                sc1 = bk_s1[s][:].rearrange("n (h m) -> n h m", m=M)
                step(v.tensor_reduce(max1[:, b, s, :], sc1, AX.X, ALU.max))
                v.tensor_tensor(d1[:, b, s], sc1, max1[:, b, s, :].unsqueeze(2).to_broadcast([P, E * J, M]),
                                ALU.subtract).then_inc(sub1_done, 1)

            def keep_pt1_last():
                dve.wait_ge(pt1_ps, HALF * LAST + 1)
                v.tensor_copy(pt1[:, LAST, 0].rearrange("m k n -> m (k n)"), bk_s1[0][:, :]).then_inc(pt1_dve, 1)

            def norm_1(b, s):
                if b < LAST:
                    dve.wait_ge(o_ps_done, HALF * (b + 1))
                else:
                    dve.wait_ge(o_ps_done, HALF * b + s + 1)
                o = o_ps[b][s].rearrange("n (e j v) -> n e j v", e=E, j=J)
                r = rsum1[:, b, s].rearrange("n (e j) -> n e j", e=E)
                step(v.reciprocal(r, o[:, :, :, D]))
                v.tensor_tensor(o_rows[:, b, s].rearrange("n j e v -> n e j v"), o[:, :, :, 0:D],
                                r.unsqueeze(3).to_broadcast([P, E, J, D]), ALU.mult).then_inc(o_kept, 1)

            def turn_o(b):
                dve.wait_ge(o_kept, HALF * (b + 1))
                v.transpose(o_cols[:, b, :], o_rows[:, b].rearrange("n s j e v -> n (s j e v)")).then_inc(o_turned, 1)

            def turn_o_last(s):
                dve.wait_ge(o_kept, HALF * LAST + s + 1)
                v.transpose(o_cols[:, LAST, s * P:(s + 1) * P],
                            o_rows[:, LAST, s].rearrange("n j e v -> n (j e v)")).then_inc(o_turned, 1)

            def result_last(s):
                dve.wait_ge(res_ps, LAST + s + 1)
                rows = slice(s * H // 2, (s + 1) * H // 2)
                v.scalar_tensor_tensor(out=res[:, LAST, s * P:(s + 1) * P], in0=res_bank_last[s][:, 0:P], scalar=l_("bo1"),
                                       in1=y[:, LAST, rows, :].rearrange("c h w -> c (h w)"), op0=ALU.add,
                                       op1=ALU.add).then_inc(res_kept, 1)

            def result(b):
                dve.wait_ge(res_ps, b + 1)
                v.scalar_tensor_tensor(out=res[:, b, :], in0=res_bank[b][:, 0:N], scalar=l_("bo1"),
                                       in1=y[:, b, 0:H, :].rearrange("c h w -> c (h w)"), op0=ALU.add,
                                       op1=ALU.add).then_inc(res_kept, 1)

            v.memset(warm[:], 0.0).then_inc(warm_clear, 1)
            keep_g(0)
            dve.wait_ge(wow_ps, 1)
            v.tensor_copy(wow[0:DH, :], bk_y[0:DH, wow_at]).then_inc(wow_kept, 1)
            dve.wait_ge(prep_in, 16)
            dve.wait_ge(rstd_ready, 1)
            v.tensor_tensor(bn_scale[:], rstd[:], p_("bn_scale"), ALU.mult)
            max_0(0, 0)
            max_0(0, 1)
            norm_0(0, 0)
            dve.wait_ge(w3_ps, 1)
            v.tensor_scalar(w3[:], bk_y[:, w3_at], p_("gamma"), None, ALU.mult).then_inc(w3_kept, 1)
            norm_0(0, 1)
            v.tensor_scalar(bn_const[:], bk_y[:, c_at], p_("gamma"), p_("bc"), ALU.mult, ALU.add).then_inc(c_kept, 1)
            keep_g(1)
            dve.wait_ge(c_kept, 1)
            step(v.tensor_tensor(bn_mid[:], bn_const[:], p_("bn_mean"), ALU.subtract))
            v.tensor_scalar(bn_bias[:], bn_mid[:], bn_scale[:], p_("bn_bias"), ALU.mult, ALU.add).then_inc(bn_ready, 1)
            max_0(1, 0)
            dve.wait_ge(late_in, 16)
            pool_1(0)
            max_0(1, 1)
            turn_q(0)
            rsum_0(1, 0)
            rsum_0(1, 1)
            bias_keys(0)
            spread_keys(0)
            keep_v(0)
            for b in range(B):
                max_sub_1(b, 0)
                max_sub_1(b, 1)
                if b == LAST:
                    keep_pt1_last()
                    keep_v(LAST)
                    result(LAST - 2)
                    result(LAST - 1)
                if b + 2 < B:
                    max_0(b + 2, 0)
                if b + 1 < B:
                    pool_1(b + 1)
                if b + 2 < B:
                    max_0(b + 2, 1)
                if b + 1 < B:
                    turn_q(b + 1)
                if 1 <= b < LAST:
                    turn_o(b - 1)
                if 2 <= b < LAST:
                    result(b - 2)
                if b + 2 < B:
                    rsum_0(b + 2, 0)
                    rsum_0(b + 2, 1)
                if b + 1 < B:
                    bias_keys(b + 1)
                    spread_keys(b + 1)
                    norm_1(b, 0)
                    norm_1(b, 1)
                if b == LAST - 1:
                    turn_o(b)
                if b + 1 < LAST:
                    keep_v(b + 1)
            for s in range(HALF):
                norm_1(LAST, s)
                turn_o_last(s)
            result_last(0)
            result_last(1)


def windows(y, b, at, n, wide):
    start = y[:, b, 0, 2 * at:2 * at + 1]
    return bass.AP(start.tensor, start.offset, [start.ap[0], (2 * W, PH), (2, n), (W, 3), (1, wide)])


_IN = ["first", "x_rest", "prep", "late"]


def packed(fields, given):
    at, n = columns(fields)
    out = np.zeros((P, n), np.float32)
    for name, a in given.items():
        out[:a.shape[0], at[name]] = a
    return out


def kernel(**inputs):
    import concourse.bacc as bacc
    from concourse.bass_utils import run_bass_kernel_spmd

    a = {k: np.asarray(v) for k, v in inputs.items()}
    l0 = {k[8:]: v for k, v in a.items() if k.startswith("L0_conv_")}
    l1 = {k[8:]: v for k, v in a.items() if k.startswith("L1_conv_")}

    def none(*shape):
        return np.zeros(shape, np.float32)

    def col(v):
        return v.reshape(-1, 1)

    sides = [np.array([3] * (n - 1) + [2]) for n in (PH, PW)]
    x_t = a["x"].reshape(B * N, C).T
    wk, wv = (l1[n].reshape(C, G, D) for n in ("w_k", "w_v"))
    bk = np.repeat(l1["b_k"].reshape(G, D).T, PP, 1)
    given = {
        "first": packed(FIRST, {
            "wfg": np.concatenate([l0["wf"], none(C, 32 - D0), l0["wg"]], 1), "bf": col(l0["bf"]),
            "bg": np.concatenate([none(32, 1), col(l0["bg"])]), "var": col(l0["bn_var"]), "x0": x_t[:, :N]}),
        "prep": packed(PREP, {
            "wo_t": l0["wo"].T, "wc1": l0["wc"][:C], "wc2": l0["wc"][C:], "wh_t": l0["wh"].T,
            "gamma": np.broadcast_to(l0["gamma"].reshape(1, 1), (P, 1)), "bc": col(l0["bc"]), "bo": col(l0["bo"]),
            "bh": col(l0["bh"]), "bn_scale": col(l0["bn_scale"]), "bn_bias": col(l0["bn_bias"]),
            "bn_mean": col(l0["bn_mean"]), "ident": np.eye(P, dtype=np.float32)}),
        "late": packed(LATE, {
            "wkv": np.concatenate([wk, none(C, G, D), none(C, G, D), wk, wv], 2).reshape(C, G * KV),
            "wq": l1["w_q"], "wo1": l1["w_o"], "bq": np.tile(l1["b_q"].reshape(I, E * D).T, (J, 1)),
            "bk": np.concatenate([bk, none(D, M), none(D, M), bk]),
            "bv": np.tile(np.repeat(l1["b_v"].reshape(G, D), PP, 0), (2, 1)),
            "inv_count": np.broadcast_to((1.0 / np.outer(*sides)).reshape(1, POOLED), (P, POOLED)),
            "bo1": col(l1["b_o"])}),
    }
    arrays = {**given, "x_rest": np.ascontiguousarray(x_t[:, N:])}
    nc = bacc.Bacc("TRN2", target_bir_lowering=False, num_devices=1)
    args = [nc.dram_tensor(f"in_{k}", arrays[k].shape, F32, kind="ExternalInput").ap() for k in _IN]
    out = nc.dram_tensor("out_t", (C, B * N), F32, kind="ExternalOutput").ap()
    build(nc, *args, out)
    r = run_bass_kernel_spmd(nc, [{f"in_{k}": arrays[k] for k in _IN}], core_ids=[0])
    return np.ascontiguousarray(r.results[0]["out_t"].T).reshape(B, H, W, C)
```
